# Optimizing a Trainium2 kernel written in Bass

```python
import numpy as np
import jax
import jax.numpy as jnp

def _softmax(x, axis=-1):
    return jax.nn.softmax(x, axis=axis)

def _gelu(x):
    return jax.nn.gelu(x, approximate=True)

def _silu(x):
    return jax.nn.silu(x)

def _sigmoid(x):
    return jax.nn.sigmoid(x)

def _layernorm(x, axis=-1, eps=1e-05):
    m = jnp.mean(x, axis=axis, keepdims=True)
    v = jnp.var(x, axis=axis, keepdims=True)
    return (x - m) / jnp.sqrt(v + eps)

def _scatter_add(tgt, idx, src, axis=0):
    return tgt.at[idx].add(src)

def _segment_sum(src, seg, n):
    return jax.ops.segment_sum(src, seg, n)
kernel_name = 'mk_decoder_preln_d1_seqx_r8_edf177'

def setup_inputs(seed: int=0):
    np.random.seed(seed)
    _w = jnp.asarray

    def _rec_inputs():
        import jax
        import jax.numpy as jnp
        _rk = jax.random.key(seed)
        x = 0.5 + 0.2887 * jax.random.normal(jax.random.fold_in(_rk, 1), (4, 256, 256), jnp.float32)
        _lenS = 256 - jax.random.randint(jax.random.fold_in(_rk, 7), (4,), 0, max(1, 256 // 4) + 1, jnp.int32)
        _lenS2 = 256 - jax.random.randint(jax.random.fold_in(_rk, 8), (4,), 0, max(1, 256 // 4) + 1, jnp.int32)
        _ctx_512P = jax.random.normal(jax.random.fold_in(_rk, 11), (4, 16, 64), jnp.float32)
        _ctx_512c = jax.random.dirichlet(jax.random.fold_in(_rk, 511), 0.3 * jnp.ones((16,), jnp.float32), (4, 256))
        _ctx_512t = jnp.einsum('bsk,bkd->bsd', _ctx_512c, _ctx_512P)
        _ctx_512t = _ctx_512t * jax.lax.rsqrt(jnp.mean(jnp.square(_ctx_512t)) + 1e-12) * 0.953939
        ctx_512 = 7.22013e-05 + 1.00017 * (_ctx_512t + 0.3 * jax.random.normal(jax.random.fold_in(_rk, 611), (4, 256, 64), jnp.float32))
        _validS = jnp.arange(256)[None, :] < _lenS[:, None]
        _validS2 = jnp.arange(256)[None, :] < _lenS2[:, None]
        _causal = jnp.tril(jnp.ones((256, 256), dtype=bool))
        mask_SxS2_bk1 = jnp.broadcast_to(_validS2[0:1, :], (256, 256))
        mask_BxS2_bf0 = jnp.logical_not(jnp.ones((4, 256), dtype=bool))
        return (x, ctx_512, mask_SxS2_bk1, mask_BxS2_bf0)
    x, ctx_512, mask_SxS2_bk1, mask_BxS2_bf0 = _rec_inputs()

    def _L0_attn_setup():
        import math
        import jax, jax.numpy as jnp
        import numpy as np
        D_MODEL = 256
        D_INNER = 512
        D_STATE = 16
        D_CONV = 4
        DT_RANK = 128
        SCALE_X = 0.05
        SCALE_CONV_OUT = 0.05

        def quant(x, scale):
            return jnp.clip(jnp.round(x / scale), -128.0, 127.0) * scale

        def fwht(x):
            d = x.shape[-1]
            shp = x.shape
            x = x.reshape(-1, d)
            h = 1
            while h < d:
                x = x.reshape(-1, d // (2 * h), 2, h)
                a, s = (x[:, :, 0, :], x[:, :, 1, :])
                x = jnp.stack([a + s, a - s], axis=2).reshape(-1, d)
                h *= 2
            return (x * d ** (-0.5)).reshape(shp)
        key = jax.random.key(seed)
        ks = jax.random.split(key, 10)
        b, l = (2, 128)
        dt0 = jnp.exp(jax.random.uniform(ks[6], (D_INNER,), minval=math.log(0.001), maxval=math.log(0.1)))
        dt_bias = dt0 + jnp.log(-jnp.expm1(-dt0))
        A = -jnp.tile(jnp.arange(1.0, D_STATE + 1.0, dtype=jnp.float32), (D_INNER, 1))
        return {'hidden_states': jax.random.normal(ks[0], (b, l, D_MODEL), jnp.float32), 'W_in': jax.random.normal(ks[1], (2 * D_INNER, D_MODEL), jnp.float32) * 0.02, 'conv_w': jax.random.normal(ks[2], (D_INNER, D_CONV), jnp.float32) * 0.2, 'conv_b': jax.random.normal(ks[3], (D_INNER,), jnp.float32) * 0.02, 'W_x': jax.random.normal(ks[4], (DT_RANK + 2 * D_STATE, D_INNER), jnp.float32) * 0.02, 'W_dt': jax.random.normal(ks[5], (D_INNER, DT_RANK), jnp.float32) * 0.02, 'dt_bias': dt_bias.astype(jnp.float32), 'A': A.astype(jnp.float32), 'D': jnp.ones((D_INNER,), jnp.float32), 'W_out': jax.random.normal(ks[7], (D_MODEL, D_INNER), jnp.float32) * 0.02}
    _L0_attn_all = _L0_attn_setup()
    _L0_attn_in = {k: v for k, v in _L0_attn_all.items() if k in ('W_in', 'conv_w', 'conv_b', 'W_x', 'W_dt', 'dt_bias', 'A', 'D', 'W_out')}
    del _L0_attn_all

    def _L0_xattn_setup():
        import jax, jax.numpy as jnp
        import numpy as np
        B, S, H = (8, 256, 64)
        key = jax.random.key(seed)
        kq, kk, kqc, kwq, kwk = jax.random.split(key, 5)
        q = jax.random.normal(kq, (B, S, H), dtype=jnp.float32)
        k = jax.random.normal(kk, (B, S, H), dtype=jnp.float32)
        qc_score = jax.random.uniform(kqc, (B, S, S), dtype=jnp.float32)
        attn_mask = jnp.triu(jnp.ones((S, S), dtype=bool), k=1)
        key_padding_mask = jnp.zeros((B, S), dtype=bool)
        scale = 1.0 / np.sqrt(H)
        Wq = jax.random.normal(kwq, (H, H), dtype=jnp.float32) * scale
        Wk = jax.random.normal(kwk, (H, H), dtype=jnp.float32) * scale
        bq = jnp.zeros((H,), dtype=jnp.float32)
        bk = jnp.zeros((H,), dtype=jnp.float32)
        return {'q': q, 'k': k, 'attn_mask': attn_mask, 'key_padding_mask': key_padding_mask, 'qc_score': qc_score, 'Wq': Wq, 'bq': bq, 'Wk': Wk, 'bk': bk}
    _L0_xattn_all = _L0_xattn_setup()
    _L0_xattn_in = {k: v for k, v in _L0_xattn_all.items() if k in ('Wq', 'bq', 'Wk', 'bk')}
    del _L0_xattn_all

    def _L0_ffn_setup():
        import jax, jax.numpy as jnp
        import numpy as np
        TOP_K = 2
        LORA_SCALE = 32.0 / 16.0
        key = jax.random.key(seed)
        ks = jax.random.split(key, 11)
        B, S, D, F, E, R = (4, 128, 256, 704, 8, 16)
        sd, sf = (1.0 / np.sqrt(D), 1.0 / np.sqrt(F))
        return {'x': jax.random.normal(ks[0], (B, S, D), jnp.float32), 'gate_w': jax.random.normal(ks[1], (E, D), jnp.float32) * 0.02, 'w1': jax.random.normal(ks[2], (F, D), jnp.float32) * sd, 'w3': jax.random.normal(ks[3], (F, D), jnp.float32) * sd, 'w2': jax.random.normal(ks[4], (D, F), jnp.float32) * sf, 'a1': jax.random.normal(ks[5], (E, R, D), jnp.float32) * sd, 'b1': jax.random.normal(ks[6], (E, F, R), jnp.float32) * 0.01, 'a3': jax.random.normal(ks[7], (E, R, D), jnp.float32) * sd, 'b3': jax.random.normal(ks[8], (E, F, R), jnp.float32) * 0.01, 'a2': jax.random.normal(ks[9], (E, R, F), jnp.float32) * sf, 'b2': jax.random.normal(ks[10], (E, D, R), jnp.float32) * 0.01}
    _L0_ffn_all = _L0_ffn_setup()
    _L0_ffn_in = {k: v for k, v in _L0_ffn_all.items() if k in ('gate_w', 'w1', 'w3', 'w2', 'a1', 'b1', 'a3', 'b3', 'a2', 'b2')}
    del _L0_ffn_all
    return {'x': x, 'ctx_512': ctx_512, 'mask_SxS2_bk1': mask_SxS2_bk1, 'mask_BxS2_bf0': mask_BxS2_bf0, 'L0_attn_W_in': _L0_attn_in['W_in'], 'L0_attn_conv_w': _L0_attn_in['conv_w'], 'L0_attn_conv_b': _L0_attn_in['conv_b'], 'L0_attn_W_x': _L0_attn_in['W_x'], 'L0_attn_W_dt': _L0_attn_in['W_dt'], 'L0_attn_dt_bias': _L0_attn_in['dt_bias'], 'L0_attn_A': _L0_attn_in['A'], 'L0_attn_D': _L0_attn_in['D'], 'L0_attn_W_out': _L0_attn_in['W_out'], 'L0_xattn_Wq': _L0_xattn_in['Wq'], 'L0_xattn_bq': _L0_xattn_in['bq'], 'L0_xattn_Wk': _L0_xattn_in['Wk'], 'L0_xattn_bk': _L0_xattn_in['bk'], 'L0_ffn_gate_w': _L0_ffn_in['gate_w'], 'L0_ffn_w1': _L0_ffn_in['w1'], 'L0_ffn_w3': _L0_ffn_in['w3'], 'L0_ffn_w2': _L0_ffn_in['w2'], 'L0_ffn_a1': _L0_ffn_in['a1'], 'L0_ffn_b1': _L0_ffn_in['b1'], 'L0_ffn_a3': _L0_ffn_in['a3'], 'L0_ffn_b3': _L0_ffn_in['b3'], 'L0_ffn_a2': _L0_ffn_in['a2'], 'L0_ffn_b2': _L0_ffn_in['b2']}

def reference(x, ctx_512, mask_SxS2_bk1, mask_BxS2_bf0, L0_attn_W_in, L0_attn_conv_w, L0_attn_conv_b, L0_attn_W_x, L0_attn_W_dt, L0_attn_dt_bias, L0_attn_A, L0_attn_D, L0_attn_W_out, L0_xattn_Wq, L0_xattn_bq, L0_xattn_Wk, L0_xattn_bk, L0_ffn_gate_w, L0_ffn_w1, L0_ffn_w3, L0_ffn_w2, L0_ffn_a1, L0_ffn_b1, L0_ffn_a3, L0_ffn_b3, L0_ffn_a2, L0_ffn_b2):
    import jax
    import jax.numpy as jnp

    def _L0_attn_ref(hidden_states, W_in, conv_w, conv_b, W_x, W_dt, dt_bias, A, D, W_out):
        import math
        import jax, jax.numpy as jnp
        import numpy as np
        D_MODEL = 256
        D_INNER = 512
        D_STATE = 16
        D_CONV = 4
        DT_RANK = 128
        SCALE_X = 0.05
        SCALE_CONV_OUT = 0.05

        def quant(x, scale):
            return jnp.clip(jnp.round(x / scale), -128.0, 127.0) * scale

        def fwht(x):
            d = x.shape[-1]
            shp = x.shape
            x = x.reshape(-1, d)
            h = 1
            while h < d:
                x = x.reshape(-1, d // (2 * h), 2, h)
                a, s = (x[:, :, 0, :], x[:, :, 1, :])
                x = jnp.stack([a + s, a - s], axis=2).reshape(-1, d)
                h *= 2
            return (x * d ** (-0.5)).reshape(shp)
        b, l, dm = hidden_states.shape
        xz = jnp.einsum('bld,ed->bel', hidden_states, W_in)
        x, z = jnp.split(xz, 2, axis=1)
        x = quant(x, SCALE_X)
        xp = jnp.pad(x, ((0, 0), (0, 0), (D_CONV - 1, 0)))
        xc = jax.lax.conv_general_dilated(xp, conv_w[:, None, :], (1,), 'VALID', dimension_numbers=('NCH', 'OIH', 'NCH'), feature_group_count=D_INNER)
        u = quant(jax.nn.silu(xc + conv_b[None, :, None]), SCALE_CONV_OUT)
        x_dbl = jnp.einsum('bdl,ed->ble', u, W_x)
        dt_in, B, C = jnp.split(x_dbl, [DT_RANK, DT_RANK + D_STATE], axis=-1)
        dt = jax.nn.softplus(jnp.einsum('blr,dr->bld', dt_in, W_dt) + dt_bias)
        xs = (dt.transpose(1, 0, 2), u.transpose(2, 0, 1), B.transpose(1, 0, 2), C.transpose(1, 0, 2))
        h0 = jnp.zeros((b, D_INNER, D_STATE), hidden_states.dtype)

        def step(h, inp):
            dt_t, u_t, B_t, C_t = inp
            dA = jnp.exp(dt_t[..., None] * A)
            h = dA * h + (dt_t * u_t)[..., None] * B_t[:, None, :]
            return (h, jnp.einsum('bdn,bn->bd', h, C_t))
        _, ys = jax.lax.scan(step, h0, xs)
        y = ys.transpose(1, 2, 0) + D[:, None] * u
        y = y * jax.nn.silu(z)
        y = fwht(y.transpose(0, 2, 1))
        return jnp.einsum('ble,de->bld', y, W_out)

    def _L0_xattn_ref(q, k, attn_mask, key_padding_mask, qc_score, Wq, bq, Wk, bk):
        import jax, jax.numpy as jnp
        import numpy as np
        B, S, H = (8, 256, 64)
        qp = jnp.einsum('bsh,oh->bso', q, Wq) + bq
        kp = jnp.einsum('bth,oh->bto', k, Wk) + bk
        scaling = jnp.asarray(float(H) ** (-0.5), dtype=qp.dtype)
        scores = jnp.einsum('bsh,bth->bst', qp, kp) * scaling
        scores = scores * qc_score
        mask = attn_mask[None, :, :] | key_padding_mask[:, None, :]
        scores = jnp.where(mask, -jnp.inf, scores)
        return jax.nn.softmax(scores, axis=-1)

    def _L0_ffn_ref(x, gate_w, w1, w3, w2, a1, b1, a3, b3, a2, b2):
        import jax, jax.numpy as jnp
        import numpy as np
        TOP_K = 2
        LORA_SCALE = 32.0 / 16.0
        B, S, D = x.shape
        E = gate_w.shape[0]
        xf = x.reshape(B * S, D)
        N = xf.shape[0]
        logits = xf @ gate_w.T
        top_w, top_i = jax.lax.top_k(logits, TOP_K)
        routing = jax.nn.softmax(top_w, axis=-1)
        w_full = jnp.zeros((N, E), x.dtype).at[jnp.arange(N)[:, None], top_i].add(routing)
        base1 = xf @ w1.T
        base3 = xf @ w3.T

        def expert_step(acc, p):
            A1, B1, A3, B3, A2, B2, we = p
            h1 = base1 + xf @ A1.T @ B1.T * LORA_SCALE
            h3 = base3 + xf @ A3.T @ B3.T * LORA_SCALE
            act = jax.nn.silu(h1) * h3
            out = act @ w2.T + act @ A2.T @ B2.T * LORA_SCALE
            return (acc + we[:, None] * out, None)
        init = jnp.zeros((N, D), x.dtype)
        out, _ = jax.lax.scan(expert_step, init, (a1, b1, a3, b3, a2, b2, w_full.T))
        return out.reshape(B, S, D)
    x = x + _L0_attn_ref(_layernorm(x, axis=-1), L0_attn_W_in, L0_attn_conv_w, L0_attn_conv_b, L0_attn_W_x, L0_attn_W_dt, L0_attn_dt_bias, L0_attn_A, L0_attn_D, L0_attn_W_out)
    x = x + _L0_xattn_ref(ctx_512, ctx_512, mask_SxS2_bk1, mask_BxS2_bf0, _layernorm(x, axis=-1), L0_xattn_Wq, L0_xattn_bq, L0_xattn_Wk, L0_xattn_bk)
    x = x + _L0_ffn_ref(_layernorm(x, axis=-1), L0_ffn_gate_w, L0_ffn_w1, L0_ffn_w3, L0_ffn_w2, L0_ffn_a1, L0_ffn_b1, L0_ffn_a3, L0_ffn_b3, L0_ffn_a2, L0_ffn_b2)
    return x

_drawn_inputs = setup_inputs


def setup_inputs(seed=0):
    import zlib

    import numpy as np

    out = dict(_drawn_inputs(seed))
    spreads = {'L0_attn_D': (1.0, 0.6), 'L0_xattn_bq': (0.0, 0.8), 'L0_xattn_bk': (0.0, 0.8)}
    factors = {'L0_attn_conv_b': 7.347,
     'L0_attn_W_x': 64.0,
     'L0_attn_W_dt': 64.0,
     'L0_attn_dt_bias': 64.0,
     'L0_attn_A': 200.0}
    for name, (base, spread) in spreads.items():
        noise = np.random.default_rng([zlib.crc32(name.encode()), seed]).standard_normal(out[name].shape)
        drawn = base * np.exp(spread * noise) if base else spread * noise
        out[name] = jnp.asarray(drawn.astype(out[name].dtype))
    for name, factor in factors.items():
        out[name] = (out[name] * factor).astype(out[name].dtype)
    return out
```

```python
from contextlib import ExitStack

import concourse.bass as bass
from concourse import mybir

F32 = mybir.dt.float32
BF16 = mybir.dt.bfloat16
U8 = mybir.dt.uint8
U32 = mybir.dt.uint32
ALU = mybir.AluOpType
ACT = mybir.ActivationFunctionType
AX = mybir.AxisListType

P = 128
BATCH, T, D = 4, 256, 256
TT = T // P
DK = D // P
DI = 512
CT = DI // P
NS = 16
NP = NS // 2
TAPS = 4
RANK = P
H = 64
E, R = 8, 16
FF = 704
FT = -(-FF // P)
EPS = 1e-5
QS = 0.05
MAGIC = 1.5 * 2.0 ** 23
MASKED = -1e30

TICKS = CT * NP
AHEAD = 1
BAHEAD = 6
XBUFS = 3
BRING = 3
TLAG = 4
CLAG = 6


def build(nc, t):
    with ExitStack() as ctx:
        def sb(name, shape, dt=F32):
            return ctx.enter_context(nc.sbuf_tensor(name, shape, dt))

        def psum(name):
            return ctx.enter_context(nc.psum_tensor(name, [P, 512], F32))

        def sems(names):
            return {n: ctx.enter_context(nc.semaphore(n)) for n in names.split()}

        ident = sb("ident", [P, P])
        identb = sb("identb", [P, P], BF16)
        had = sb("had", [P, P])
        sel = sb("sel", [P, NS, P], BF16)
        rank_expert = sb("rank_expert", [P, P])
        w_in = sb("w_in", [P, DK, 2 * DI])
        conv_w = sb("conv_w", [P, CT, TAPS])
        conv_ws = sb("conv_ws", [P, CT, TAPS])
        conv_b = sb("conv_b", [P, CT])
        WX = 2 * P + NS
        w_x3 = [sb(f"w_x3_{i}", [P, CT, WX], BF16) for i in range(3)]
        w_dt = sb("w_dt", [P, DI])
        dt_bias = sb("dt_bias", [P, CT])
        a_log = sb("a_log", [P, CT, NS])
        d_skip = sb("d_skip", [P, CT])
        w_oh = sb("w_oh", [P, CT, D])
        ctx_t = sb("ctx_t", [H, BATCH, T])
        w_q = sb("w_q", [H, H])
        w_k = sb("w_k", [H, H])
        b_qk = sb("b_qk", [H, 2])
        masked = sb("masked", [P, BATCH, TT, T], U8)
        gate = sb("gate", [P, DK, E])
        w1 = sb("w1", [P, DK, FT * P])
        w3 = sb("w3", [P, DK, FT * P])
        w2 = sb("w2", [P, FT, D])
        la1 = sb("la1", [P, DK, P])
        la3 = sb("la3", [P, DK, P])
        lb1 = sb("lb1", [P, FT * P])
        lb3 = sb("lb3", [P, FT * P])
        la2 = sb("la2", [P, FT, P])
        lb2 = sb("lb2", [P, D])

        minus_half = sb("minus_half", [P, TT])

        x_t = [sb(f"x_t{i}", [P, TT, D]) for i in range(XBUFS)]
        f_st = sb("f_st", [P, TT, 6])
        f_mv = sb("f_mv", [P, TT, 2])
        f_rs = sb("f_rs", [P, TT])
        xn = sb("xn", [P, TT, D])
        xn_t = sb("xn_t", [P, DK, T])
        q = sb("q", [P, CT, TAPS - 1 + T], BF16)
        v = sb("v", [P, CT, T])
        th = sb("th", [P, CT, T])
        zs = [sb(f"zs{i}", [P, CT, T]) for i in range(2)]
        u = [sb(f"u{i}", [P, CT, T], BF16) for i in range(2)]
        dt_in = sb("dt_in", [P, T])
        b_hi = [sb(f"b_hi{i}", [P, T], BF16) for i in range(2)]
        b_rest = sb("b_rest", [P, T])
        b_mid = sb("b_mid", [P, T], BF16)
        c_t = [sb(f"c_t{i}", [P, TT, NS]) for i in range(2)]
        dt_abs = sb("dt_abs", [P, CT, T])
        xq = dt_abs
        dt_pos = v
        dt = [sb(f"dt{i}", [P, CT, T]) for i in range(2)]
        dtu = [sb(f"dtu{i}", [P, CT, T]) for i in range(2)]

        b_rep = sb("b_rep", [P, BRING, 2, T])
        bu = sb("bu", [P, 3, 2, T])
        h = sb("h", [P, 2, CT, 2, T])
        acc = [sb(f"acc{i}", [P, TT, DI]) for i in range(2)]

        yd = sb("yd", [P, CT, T])
        x1 = sb("x1", [P, TT, D])
        qk = sb("qk", [H, 2, T])
        sc = sb("sc", [P, TT, T])
        a_st = sb("a_st", [P, TT, 6])
        a_mv = sb("a_mv", [P, TT, 2])
        a_rs = sb("a_rs", [P, TT])
        a_mx = sb("a_mx", [P, TT])
        a_nm = sb("a_nm", [P, TT])
        a_sum = sb("a_sum", [P, TT])
        a_rec = sb("a_rec", [P, TT])
        x2 = sb("x2", [P, TT, D])
        n_st = sb("n_st", [P, TT, 6])
        n_mv = sb("n_mv", [P, TT, 2])
        n_rs = sb("n_rs", [P, TT])
        xf = sb("xf", [P, TT, D])
        qc = xf
        xf_t = sb("xf_t", [P, DK, T])
        lg = sb("lg", [P, TT, E])
        top = sb("top", [P, TT, 8])
        topi = sb("topi", [P, TT, 8], U32)
        topf = sb("topf", [P, TT, 8])
        g_d = sb("g_d", [P, TT])
        g_ex = sb("g_ex", [P, TT])
        g_one = sb("g_one", [P, TT])
        g_rec = sb("g_rec", [P, TT])
        g_w = sb("g_w", [P, 2, TT])
        hot = sb("hot", [P, 2, TT, P], BF16)
        hot_t = sb("hot_t", [P, 2, T])
        w_rep = sb("w_rep", [P, 2, T])
        xa1 = sb("xa1", [P, 2, T])
        xad = sb("xad", [P, 2, T])
        ht = sb("ht", [P, 2, T])
        h3 = sb("h3", [P, 2, T])
        hot_d = h3[:, 0, :]
        hg = sb("hg", [P, 2, T])
        aw = sb("aw", [P, FT, 2, T])
        aws = sb("aws", [P, FT, T])
        p_m = xa1
        p_s = ht[:, 0, :]
        xo = sb("xo", [P, TT, D])
        w_x, w_xr = (h[:, i, :, :, :].rearrange("p c n t -> p (c n t)")[:, 0:CT * WX].rearrange(
            "p (c n) -> p c n", c=CT) for i in range(2))
        mask = aws[:, 0:1, 0:TT * T // 4].bitcast(U8).rearrange("p o (a t) -> p (o a) t", a=TT)
        kmask = aws[:, 1:2, 0:BATCH * T // 4].bitcast(U8).rearrange("p o (b t) -> p (o b) t", b=BATCH)
        w_out, w_bf = (aw[:, 2 * i:2 * i + 2, :, :].rearrange("p f i t -> p (f i) t") for i in range(2))

        decay = [psum(f"decay{i}") for i in range(2)]
        h_t = [psum(f"h_t{i}") for i in range(2)]
        b_ps = psum("b_ps")
        f_ps = psum("f_ps")
        r_ps = [psum(f"r_ps{i}") for i in range(2)]

        s = sems(
            "ld_x0 ld_x1 ld_x2 ld_id ld_in ld_conv ld_x ld_sel ld_out ld_att ld_ffn stored "
            "half_set eps_added pads_set taps_set wx_hi wx_rest wx_mid wx_lo had_sum had_mm had_done masks_set "
            "f_var f_rstd f_xn f_turned f_xn_t f_proj f_xcopy f_quant f_tap f_conv f_ztanh f_z "
            "f_vtanh f_u f_xproj f_cproj f_dtin f_bhi f_brest f_bmid f_bsplit f_c f_dtproj "
            "f_abs f_pos f_exp f_ln f_dt f_dtu "
            "b_spread b_copied bu_ready decay_ready scanned turned weighted "
            "o_turned o_skip o_gated o_mm o_x1 a_qkmm a_qk a_scmm a_sc a_var a_rstd a_max a_exp a_x2 "
            "n_var n_rstd n_xf n_turned n_xft g_mm g_xa g_diff g_exp g_wts g_hot g_hturned g_hcopy "
            "g_wturned g_wcopy g_xa1 g_xad h_mm h_tanh h_copy h_gate h_pair h_act h_sum p_mm p_mask "
            "p_sum e_mm e_done "
            "dve_done")
        ld_xt = [s["ld_x0"], s["ld_x1"], s["ld_x2"]]

        def pair(bank, i=None):
            v2 = bank[:, :].rearrange("p (a t) -> p a t", a=2)
            return v2 if i is None else v2[:, i, :]

        def front_at(slot):
            return slot + 1 if 0 <= slot + 1 < BATCH else None

        def rest_at(slot):
            return slot - 1 if 0 <= slot - 1 < BATCH else None

        def step(tick, offset):
            k = tick - offset
            return k if 0 <= k < BATCH * TICKS else None

        SLOTS = range(-1, BATCH + 1)
        block = ctx.enter_context(nc.Block())

        @block.sync
        def _(sp):
            def x_load(b):
                sp.dma_start(x_t[b % XBUFS][:, :, :],
                             t["x"][b].rearrange("(a p) d -> p a d", p=P)).then_inc(ld_xt[b % XBUFS], 16)

            x_load(0)
            sp.dma_start(ident[:, :], t["ident"]).then_inc(s["ld_id"], 16)
            sp.dma_start(w_in[:, :, :], t["w_in"]).then_inc(s["ld_in"], 16)
            for dst, name in ((conv_w[:, :, :], "conv_w"), (conv_b[:, :], "conv_b"), (d_skip[:, :], "d_skip"),
                              (a_log[:, :, :], "a_log"), (dt_bias[:, :], "dt_bias")):
                sp.dma_start(dst, t[name]).then_inc(s["ld_conv"], 16)
            sp.dma_start(w_x[:, :, :], t["w_x"]).then_inc(s["ld_x"], 16)
            sp.dma_start(w_dt[:, :], t["w_dt"]).then_inc(s["ld_x"], 16)
            sp.dma_start(sel[:, :, :], t["sel"]).then_inc(s["ld_sel"], 16)
            sp.dma_start(w_out[:, :, :], t["w_out"]).then_inc(s["ld_out"], 16)
            sp.dma_start(had[:, :], t["had"]).then_inc(s["ld_out"], 16)
            x_load(1)
            x_load(2)
            for dst, name in ((ctx_t[:, :, :], "ctx_t"), (w_q[:, :], "w_q"), (w_k[:, :], "w_k"),
                              (b_qk[:, :], "b_qk"), (mask[:, :, :], "mask"), (kmask[:, :, :], "kmask")):
                sp.dma_start(dst, t[name]).then_inc(s["ld_att"], 16)
            for dst, name in ((gate[:, :, :], "gate"), (la1[:, :, :], "la1"), (la3[:, :, :], "la3"),
                              (rank_expert[:, :], "rank_expert"), (identb[:, :], "identb"),
                              (w1[:, :, :], "w1"), (w3[:, :, :], "w3"), (lb1[:, :], "lb1"), (lb3[:, :], "lb3"),
                              (w2[:, :, :], "w2"), (la2[:, :, :], "la2"), (lb2[:, :], "lb2")):
                sp.dma_start(dst, t[name]).then_inc(s["ld_ffn"], 16)
            for b in range(BATCH):
                if b + XBUFS < BATCH:
                    sp.wait_ge(s["o_x1"], b + 1)
                    x_load(b + XBUFS)
                sp.wait_ge(s["e_done"], b + 1)
                sp.dma_start(t["out"][b].rearrange("(a p) d -> p a d", p=P),
                             xo[:, :, :]).then_inc(s["stored"], 16)
            sp.wait_ge(s["stored"], 16 * BATCH)

        LOADED_CONV, LOADED_X, LOADED_OUT, LOADED_ATT, LOADED_FFN = 5 * 16, 2 * 16, 2 * 16, 6 * 16, 12 * 16

        @block.tensor
        def _(pe):
            mm, turn = nc.tensor.matmul, nc.tensor.transpose

            def hadamard_out():
                pe.wait_ge(s["ld_out"], LOADED_OUT)
                pe.wait_ge(s["had_sum"], 4)
                for j in range(CT):
                    last = mm(pair(r_ps[j // 2], j % 2), had[:, :], w_bf[:, j, :], start=True, stop=True)
                    if j % 2:
                        last.then_inc(s["had_mm"], 1)

            def f_turn(b):
                pe.wait_ge(s["ld_id"], 16)
                pe.wait_ge(s["f_xn"], b + 1)
                if b:
                    pe.wait_ge(s["f_pos"], 2 * b)
                    pe.wait_ge(s["f_abs"], 2 * b)
                for k in range(DK):
                    for a in range(TT):
                        last = turn(pair(f_ps, k)[:, a * P:a * P + P], xn[:, a, k * P:k * P + P], ident[:, :])
                last.then_inc(s["f_turned"], 1)

            def f_proj(b, i):
                pe.wait_ge(s["ld_in"], 16)
                pe.wait_ge(s["f_xn_t"], b + 1)
                if i in (1, 2):
                    pe.wait_ge(s["f_xcopy"], 2 * b + i)
                if i == 3:
                    pe.wait_ge(s["f_ztanh"], 2 * b + 1)
                    pe.wait_ge(s["f_z"], 2 * b + 1)
                for j in range(2):
                    c = 2 * i + j
                    for k in range(DK):
                        last = mm(pair(f_ps, j), w_in[:, k, c * P:c * P + P], xn_t[:, k, :],
                                  start=(k == 0), stop=(k == DK - 1))
                last.then_inc(s["f_proj"], 1)

            def f_xproj(b):
                pe.wait_ge(s["wx_lo"], 1)
                pe.wait_ge(s["f_u"], b + 1)
                pe.wait_ge(s["f_ztanh"], 2 * b + 2)
                pe.wait_ge(s["f_z"], 2 * b + 2)
                for j in range(2):
                    n = 0
                    for k in range(CT):
                        for part in w_x3:
                            last = mm(pair(f_ps, j), part[:, k, j * P:j * P + P], u[b % 2][:, k, :],
                                      start=(n == 0), stop=(n == 3 * CT - 1))
                            n += 1
                last.then_inc(s["f_xproj"], 1)

            def f_cproj(b):
                pe.wait_ge(s["f_dtin"], b + 1)
                pe.wait_ge(s["f_bhi"], b + 1)
                pe.wait_ge(s["f_brest"], b + 1)
                for a in range(TT):
                    n = 0
                    for k in range(CT):
                        for part in w_x3:
                            last = mm(f_ps[:, a * NS:a * NS + NS], u[b % 2][:, k, a * P:a * P + P],
                                      part[:, k, 2 * P:2 * P + NS], start=(n == 0), stop=(n == 3 * CT - 1))
                            n += 1
                last.then_inc(s["f_cproj"], 1)

            def f_dtproj(b, i):
                pe.wait_ge(s["ld_x"], LOADED_X)
                pe.wait_ge(s["f_dtin"], b + 1)
                if i == 0:
                    pe.wait_ge(s["f_c"], b + 1)
                else:
                    pe.wait_ge(s["f_abs"], 2 * b + 1)
                    pe.wait_ge(s["f_pos"], 2 * b + 1)
                for j in range(2):
                    c = 2 * i + j
                    last = mm(pair(f_ps, j), w_dt[:, c * P:c * P + P], dt_in[:, :], start=True, stop=True)
                last.then_inc(s["f_dtproj"], 1)

            def spread_b(g):
                b, n = g // NP, g % NP
                pe.wait_ge(s["ld_sel"], 16)
                pe.wait_ge(s["f_bsplit"], b + 1)
                if g:
                    pe.wait_ge(s["b_copied"], g)
                for j in range(2):
                    last = mm(pair(b_ps, j), sel[:, 2 * n + j, :], b_hi[b % 2][:, :], start=True, stop=True)
                last.then_inc(s["b_spread"], 1)

            def turn_h(k):
                g, n, a = k // 4, (k // 2) % 2, k % 2
                pe.wait_ge(s["scanned"], 4 * g + 4)
                if k >= 2:
                    pe.wait_ge(s["weighted"], k - 1)
                for c in range(CT):
                    last = turn(h_t[k % 2][:, c * P:c * P + P], h[:, g % 2, c, n, a * P:a * P + P], ident[:, :])
                last.then_inc(s["turned"], 1)

            def a_qk(b):
                pe.wait_ge(s["ld_att"], LOADED_ATT)
                if b == 0:
                    pe.wait_ge(s["had_done"], 1)
                else:
                    pe.wait_ge(s["e_done"], b)
                for i, w in enumerate((w_q, w_k)):
                    last = mm(pair(r_ps[0], i)[0:H, :], w[:, :], ctx_t[:, b, :], start=True, stop=True)
                last.then_inc(s["a_qkmm"], 1)

            def a_scores(b):
                pe.wait_ge(s["a_qk"], 2 * b + 2)
                if b == 0:
                    pe.wait_ge(s["had_done"], 2)
                else:
                    pe.wait_ge(s["p_mask"], b)
                for a in range(TT):
                    last = mm(pair(r_ps[1], a), qk[:, 0, a * P:a * P + P], qk[:, 1, :], start=True, stop=True)
                last.then_inc(s["a_scmm"], 1)

            def o_turn(b):
                pe.wait_ge(s["weighted"], TICKS * (b + 1))
                pe.wait_ge(s["a_sc"], b + 1)
                for i in range(2):
                    for j in range(2):
                        for a in range(TT):
                            c = 2 * i + j
                            last = turn(pair(r_ps[i], j)[:, a * P:a * P + P],
                                        acc[b % 2][:, a, c * P:c * P + P], ident[:, :])
                    last.then_inc(s["o_turned"], 1)

            def o_proj(b):
                pe.wait_ge(s["o_gated"], 2 * b + 2)
                for a in range(TT):
                    for c in range(CT):
                        last = mm(pair(r_ps[0], a), yd[:, c, a * P:a * P + P], w_oh[:, c, :],
                                  start=(c == 0), stop=(c == CT - 1))
                last.then_inc(s["o_mm"], 1)

            def n_turn(b):
                pe.wait_ge(s["n_xf"], b + 1)
                for k in range(DK):
                    for a in range(TT):
                        last = turn(pair(r_ps[1], k)[:, a * P:a * P + P], xf[:, a, k * P:k * P + P], ident[:, :])
                last.then_inc(s["n_turned"], 1)

            def g_logits(b):
                pe.wait_ge(s["ld_ffn"], LOADED_FFN)
                pe.wait_ge(s["n_xft"], b + 1)
                pe.wait_ge(s["o_x1"], b + 1)
                for a in range(TT):
                    for k in range(DK):
                        last = mm(r_ps[0][:, a * E:a * E + E], xf_t[:, k, a * P:a * P + P], gate[:, k, :],
                                  start=(k == 0), stop=(k == DK - 1))
                last.then_inc(s["g_mm"], 1)

            def g_lora(b):
                for i, w in enumerate((la1, la3)):
                    for k in range(DK):
                        last = mm(pair(r_ps[1], i), w[:, k, :], xf_t[:, k, :], start=(k == 0), stop=(k == DK - 1))
                last.then_inc(s["g_xa"], 1)

            def g_turn_hot(b):
                pe.wait_ge(s["g_hot"], b + 1)
                hb = r_ps[0][:, 0:256].bitcast(BF16).rearrange("p (s t) -> p s t", s=2)
                for i in range(2):
                    for a in range(TT):
                        last = turn(hb[:, i, a * P:a * P + P], hot[:, i, a, :], identb[:, :])
                last.then_inc(s["g_hturned"], 1)

            def g_turn_w(b):
                pe.wait_ge(s["g_wts"], b + 1)
                pe.wait_ge(s["g_hcopy"], b + 1)
                for i in range(2):
                    for a in range(TT):
                        last = turn(pair(r_ps[0], i)[:, a * P:a * P + P],
                                    g_w[:, i, a:a + 1].to_broadcast([P, P]), ident[:, :])
                last.then_inc(s["g_wturned"], 1)

            def ffn_up(b, j):
                f, i = 2 * (j // 4) + j % 2, (j // 2) % 2
                bank = r_ps[(f + 1) % 2]
                n = FT * 2 * b
                if i == 0:
                    if f == 0:
                        pe.wait_ge(s["g_xa1"], b + 1)
                        pe.wait_ge(s["g_xad"], b + 1)
                    elif f == 1:
                        pe.wait_ge(s["g_wcopy"], b + 1)
                if i == 1 or f >= 2:
                    pe.wait_ge(s["h_gate"], n + j - 1)
                    pe.wait_ge(s["h_copy"], n + j - 1)
                for o, (w, lb) in enumerate(((w1, lb1), (w3, lb3))):
                    if i == 0:
                        for k in range(DK):
                            mm(pair(bank, o), w[:, k, f * P:f * P + P], xf_t[:, k, :],
                               start=(k == 0 and o == 0), stop=False, skip_group_check=True)
                    last = mm(pair(bank, o), lb[:, f * P:f * P + P], (xad if i else xa1)[:, o, :],
                              start=False, stop=True, skip_group_check=True)
                last.then_inc(s["h_mm"], 1)

            def ffn_ranks(b):
                pe.wait_ge(s["h_act"], 12 * b + 12)
                pe.wait_ge(s["h_gate"], 12 * b + 12)
                pe.wait_ge(s["h_copy"], 12 * b + 12)
                for f in range(FT):
                    last = mm(r_ps[1][:, :], la2[:, f, :], aw[:, f, :, :], start=(f == 0), stop=(f == FT - 1))
                last.then_inc(s["p_mm"], 1)

            def ffn_down(b):
                pe.wait_ge(s["h_sum"], FT * b + FT)
                for a in range(TT):
                    for f in range(FT):
                        mm(pair(r_ps[0], a), aws[:, f, a * P:a * P + P], w2[:, f, :],
                           start=(f == 0 and a == 0), stop=False, skip_group_check=True)
                pe.wait_ge(s["p_sum"], b + 1)
                for a in range(TT):
                    last = mm(pair(r_ps[0], a), p_s[:, a * P:a * P + P], lb2[:, :],
                              start=False, stop=True, skip_group_check=True)
                last.then_inc(s["e_mm"], 1)

            for slot in SLOTS:
                f, r = front_at(slot), rest_at(slot)
                for k in range(TICKS):
                    tick = slot * TICKS + k
                    if (st := step(tick, -BAHEAD)) is not None and st % 4 == 0:
                        spread_b(st // 4)
                    if (st := step(tick, TLAG)) is not None:
                        turn_h(st)
                    if f is not None:
                        if k == 2:
                            f_turn(f)
                        if 3 <= k < 5:
                            f_proj(f, k - 3)
                        if 10 <= k < 12:
                            f_proj(f, k - 8)
                        if k == 15:
                            f_xproj(f)
                        if k == 18:
                            f_cproj(f)
                        if 19 <= k < 21:
                            f_dtproj(f, k - 19)
                    if slot == -1 and k == 22:
                        hadamard_out()
                    if r is not None:
                        if k == 0:
                            a_qk(r)
                        if k == 1:
                            a_scores(r)
                        if k == 6:
                            o_turn(r)
                        if k == 9:
                            o_proj(r)
                        if k == 15:
                            n_turn(r)
                        if k == 16:
                            g_logits(r)
                            g_lora(r)
                        if k == 18:
                            g_turn_hot(r)
                            g_turn_w(r)
                        if 19 <= k < 31:
                            ffn_up(r, k - 19)
                        if k == 31:
                            ffn_ranks(r)
                            ffn_down(r)

        @block.scalar
        def _(act):
            go = nc.scalar.activation

            def split_wx():
                act.wait_ge(s["ld_x"], LOADED_X)
                go(w_x3[0][:, :, :], w_x[:, :, :], ACT.Copy).then_inc(s["wx_hi"], 1)
                act.wait_ge(s["wx_rest"], 1)
                go(w_x3[1][:, :, :], w_xr[:, :, :], ACT.Copy).then_inc(s["wx_mid"], 1)

            def hadamard_out():
                for i in range(2):
                    act.wait_ge(s["had_mm"], i + 1)
                    go(w_oh[:, 2 * i:2 * i + 2, :], pair(r_ps[i]), ACT.Copy,
                       scale=DI ** -0.5 * QS * 0.5).then_inc(s["had_done"], 1)

            def f_xn_copy(b):
                act.wait_ge(s["f_turned"], b + 1)
                go(xn_t[:, :, :], pair(f_ps), ACT.Copy).then_inc(s["f_xn_t"], 1)

            def f_xcopy(b, i):
                act.wait_ge(s["f_proj"], 4 * b + i + 1)
                go(xq[:, 2 * i:2 * i + 2, :], pair(f_ps), ACT.Copy, scale=1.0 / QS).then_inc(s["f_xcopy"], 1)

            def f_ztanh(b, i):
                act.wait_ge(s["f_proj"], 4 * b + i + 3)
                go(th[:, 2 * i:2 * i + 2, :], pair(f_ps), ACT.Tanh, scale=0.5).then_inc(s["f_ztanh"], 1)

            def f_tap(b, c):
                act.wait_ge(s["taps_set"], 1)
                act.wait_ge(s["f_quant"], 2 * b + c // 2 + 1)
                if b:
                    act.wait_ge(s["f_u"], b)
                go(v[:, c, :], q[:, c, TAPS - 1:TAPS - 1 + T], ACT.Identity, bias=conv_b[:, c:c + 1],
                   scale=conv_ws[:, c, TAPS - 1:TAPS]).then_inc(s["f_tap"], 1)

            def f_vtanh(b):
                act.wait_ge(s["f_conv"], 4 * b + 4)
                act.wait_ge(s["f_z"], 2 * b + 2)
                go(th[:, :, :], v[:, :, :], ACT.Tanh, scale=0.5).then_inc(s["f_vtanh"], 1)

            def f_split(b):
                act.wait_ge(s["f_xproj"], b + 1)
                go(b_hi[b % 2][:, :], pair(f_ps, 1), ACT.Copy).then_inc(s["f_bhi"], 1)
                go(dt_in[:, :], pair(f_ps, 0), ACT.Copy, scale=QS).then_inc(s["f_dtin"], 1)

            def f_split2(b):
                act.wait_ge(s["f_brest"], b + 1)
                go(b_mid[64:96, :], b_rest[64:96, :], ACT.Copy)
                go(b_hi[b % 2][32:64, :], b_rest[32:64, :], ACT.Copy).then_inc(s["f_bmid"], 1)

            def f_ccopy(b):
                act.wait_ge(s["f_cproj"], b + 1)
                go(c_t[b % 2][:, :, :], f_ps[:, 0:TT * NS].rearrange("p (a n) -> p a n", a=TT),
                   ACT.Copy).then_inc(s["f_c"], 1)

            def f_abs(b, i):
                act.wait_ge(s["f_dtproj"], 2 * b + i + 1)
                for j in range(2):
                    c = 2 * i + j
                    last = go(dt_abs[:, c, :], pair(f_ps, j), ACT.Abs, bias=dt_bias[:, c:c + 1])
                last.then_inc(s["f_abs"], 1)

            def f_softplus(b):
                act.wait_ge(s["f_abs"], 2 * b + 2)
                go(dt_abs[:, :, :], dt_abs[:, :, :], ACT.Exp, scale=-1.0).then_inc(s["f_exp"], 1)
                act.wait_ge(s["f_exp"], b + 1)
                go(dt_abs[:, :, :], dt_abs[:, :, :], ACT.Ln, bias=1.0).then_inc(s["f_ln"], 1)

            def copy_b(g):
                act.wait_ge(s["b_spread"], g + 1)
                if g >= BRING:
                    act.wait_ge(s["bu_ready"], 4 * (g - BRING + 1))
                go(b_rep[:, g % BRING, :, :], pair(b_ps), ACT.Copy).then_inc(s["b_copied"], 1)

            def decays(k):
                b, n, c = k // TICKS, (k // 4) % NP, k % 4
                act.wait_ge(s["f_dt"], b + 1)
                act.wait_ge(s["pads_set"], 1)
                if k >= 2:
                    act.wait_ge(s["scanned"], k - 1)
                for j in range(2):
                    last = go(pair(decay[k % 2], j)[:, 1:T], dt[b % 2][:, c, 1:T], ACT.Exp,
                              scale=a_log[:, c, 2 * n + j:2 * n + j + 1])
                last.then_inc(s["decay_ready"], 1)

            def a_qk(b):
                act.wait_ge(s["a_qkmm"], b + 1)
                for i in range(2):
                    go(qk[:, i, :], pair(r_ps[0], i)[0:H, :], ACT.Identity,
                       bias=b_qk[:, i:i + 1]).then_inc(s["a_qk"], 1)

            def a_scores(b):
                act.wait_ge(s["a_scmm"], b + 1)
                if b:
                    act.wait_ge(s["a_x2"], b)
                go(sc[:, :, :], pair(r_ps[1]), ACT.Copy, scale=H ** -0.5).then_inc(s["a_sc"], 1)

            def a_probs(b):
                act.wait_ge(s["a_max"], b + 1)
                for a in range(TT):
                    last = go(sc[:, a, :], sc[:, a, :], ACT.Exp, bias=a_nm[:, a:a + 1],
                              accum_out=a_sum[:, a:a + 1])
                last.then_inc(s["a_exp"], 1)

            def n_copy(b):
                act.wait_ge(s["n_turned"], b + 1)
                go(xf_t[:, :, :], pair(r_ps[1]), ACT.Copy).then_inc(s["n_xft"], 1)

            def g_exp(b):
                act.wait_ge(s["g_diff"], b + 1)
                go(g_ex[:, :], g_d[:, :], ACT.Exp).then_inc(s["g_exp"], 1)

            def g_copies(b):
                act.wait_ge(s["g_hturned"], b + 1)
                go(hot_t[:, :, :], r_ps[0][:, 0:256].bitcast(BF16).rearrange("p (s t) -> p s t", s=2),
                   ACT.Copy).then_inc(s["g_hcopy"], 1)
                act.wait_ge(s["g_wturned"], b + 1)
                go(w_rep[:, :, :], pair(r_ps[0]), ACT.Copy).then_inc(s["g_wcopy"], 1)

            def ffn_act(b, j):
                f, n = 2 * (j // 4) + j % 2, 12 * b
                bank = r_ps[(f + 1) % 2]
                act.wait_ge(s["h_mm"], n + j + 1)
                if n + j >= 2:
                    act.wait_ge(s["h_gate"], n + j - 1)
                go(ht[:, j % 2, :], pair(bank, 0), ACT.Tanh, scale=0.5).then_inc(s["h_tanh"], 1)
                if n + j >= 2:
                    act.wait_ge(s["h_pair"], n + j - 1)
                go(h3[:, j % 2, :], pair(bank, 1), ACT.Copy).then_inc(s["h_copy"], 1)

            for slot in SLOTS:
                f, r = front_at(slot), rest_at(slot)
                for k in range(TICKS):
                    tick = slot * TICKS + k
                    if (st := step(tick, -BAHEAD)) is not None and st % 4 == 0:
                        copy_b(st // 4)
                    if (st := step(tick, -AHEAD)) is not None:
                        decays(st)
                    if slot == -1 and k == 0:
                        split_wx()
                    if slot == -1 and k == 22:
                        hadamard_out()
                    if f is not None:
                        if k == 2:
                            f_xn_copy(f)
                        if 3 <= k < 5:
                            f_xcopy(f, k - 3)
                        if 10 <= k < 12:
                            f_ztanh(f, k - 10)
                        if 6 <= k < 10:
                            f_tap(f, k - 6)
                        if k == 12:
                            f_vtanh(f)
                        if k == 15:
                            f_split(f)
                        if k == 17:
                            f_split2(f)
                        if k == 18:
                            f_ccopy(f)
                        if 19 <= k < 21:
                            f_abs(f, k - 19)
                        if k == 21:
                            f_softplus(f)
                    if r is not None:
                        if k == 0:
                            a_qk(r)
                        if k == 1:
                            a_scores(r)
                        if k == 12:
                            a_probs(r)
                        if k == 15:
                            n_copy(r)
                        if k == 17:
                            g_exp(r)
                        if k == 18:
                            g_copies(r)
                        if 19 <= k < 31:
                            ffn_act(r, k - 19)

        @block.gpsimd
        def _(pool):
            tt, ts = nc.gpsimd.tensor_tensor, nc.gpsimd.tensor_scalar

            count = [0]

            def rstd(out, mv):
                count[0] += 1
                ts(out[:, :], mv[:, :, 1], EPS, None, ALU.add).then_inc(s["eps_added"], 1)
                pool.wait_ge(s["eps_added"], count[0])
                return tt(out[:, :], out[:, :], minus_half[:, :], ALU.pow)

            def hadamard4():
                pool.wait_ge(s["ld_out"], LOADED_OUT)
                tmp = yd
                tt(tmp[:, 0::2, :], w_out[:, 0::2, :], w_out[:, 1::2, :], ALU.add).then_inc(s["had_sum"], 1)
                tt(tmp[:, 1::2, :], w_out[:, 0::2, :], w_out[:, 1::2, :], ALU.subtract).then_inc(s["had_sum"], 1)
                pool.wait_ge(s["had_sum"], 2)
                tt(w_bf[:, 0:2, :], tmp[:, 0:2, :], tmp[:, 2:4, :], ALU.add).then_inc(s["had_sum"], 1)
                tt(w_bf[:, 2:4, :], tmp[:, 0:2, :], tmp[:, 2:4, :], ALU.subtract).then_inc(s["had_sum"], 1)

            def scan_input(k):
                b, g, c = k // TICKS, k // 4, k % 4
                pool.wait_ge(s["b_copied"], g + 1)
                pool.wait_ge(s["f_dtu"], b + 1)
                if k >= 3:
                    pool.wait_ge(s["scanned"], k - 2)
                tt(bu[:, k % 3, :, :], b_rep[:, g % BRING, :, :], dtu[b % 2][:, c:c + 1, :].to_broadcast([P, 2, T]),
                   ALU.mult).then_inc(s["bu_ready"], 1)

            def o_gate(b, i):
                pool.wait_ge(s["o_skip"], 2 * b + i + 1)
                tt(yd[:, 2 * i:2 * i + 2, :], yd[:, 2 * i:2 * i + 2, :], zs[b % 2][:, 2 * i:2 * i + 2, :],
                   ALU.mult).then_inc(s["o_gated"], 1)

            def ffn_pair(b, j):
                f, i, n = 2 * (j // 4) + j % 2, (j // 2) % 2, 12 * b
                pool.wait_ge(s["h_gate"], n + j + 1)
                pool.wait_ge(s["h_copy"], n + j + 1)
                if n + j >= 2:
                    pool.wait_ge(s["h_act"], n + j - 1)
                tt(hg[:, j % 2, :], hg[:, j % 2, :], h3[:, j % 2, :], ALU.mult).then_inc(s["h_pair"], 1)
                pool.wait_ge(s["h_pair"], n + j + 1)
                pool.wait_ge(s["g_wcopy"], b + 1)
                if b:
                    pool.wait_ge(s["p_mm"], b)
                tt(aw[:, f, i, :], hg[:, j % 2, :], w_rep[:, i, :], ALU.mult).then_inc(s["h_act"], 1)
                if i == 1:
                    pool.wait_ge(s["h_act"], n + j + 1)
                    if b:
                        pool.wait_ge(s["e_mm"], b)
                    tt(aws[:, f, :], aw[:, f, 0, :], aw[:, f, 1, :], ALU.add).then_inc(s["h_sum"], 1)

            def p_sum(b):
                pool.wait_ge(s["p_mask"], b + 1)
                tt(p_s, p_m[:, 0, :], p_m[:, 1, :], ALU.add).then_inc(s["p_sum"], 1)

            nc.gpsimd.memset(minus_half[:, :], -0.5).then_inc(s["half_set"], 1)
            pool.wait_ge(s["half_set"], 1)
            for slot in SLOTS:
                f, r = front_at(slot), rest_at(slot)
                for k in range(TICKS):
                    tick = slot * TICKS + k
                    if (st := step(tick, -AHEAD)) is not None:
                        scan_input(st)
                    if f is not None and k == 0:
                        pool.wait_ge(s["f_var"], f + 1)
                        rstd(f_rs, f_mv).then_inc(s["f_rstd"], 1)
                    if slot == -1 and k == 1:
                        hadamard4()
                    if r is not None:
                        if k == 7:
                            o_gate(r, 0)
                        if k == 8:
                            o_gate(r, 1)
                        if k == 10:
                            pool.wait_ge(s["a_var"], r + 1)
                            rstd(a_rs, a_mv).then_inc(s["a_rstd"], 1)
                        if k == 13:
                            pool.wait_ge(s["n_var"], r + 1)
                            rstd(n_rs, n_mv).then_inc(s["n_rstd"], 1)
                        if 20 <= k < 32:
                            ffn_pair(r, k - 20)
                        if k == 31:
                            p_sum(r)

        @block.vector
        def _(dve):
            ve = nc.vector
            tt, ts, stt = ve.tensor_tensor, ve.tensor_scalar, ve.scalar_tensor_tensor
            done = [0]

            def mark(ins):
                done[0] += 1
                ins.then_inc(s["dve_done"], 1)
                return done[0]

            def after(n):
                dve.wait_ge(s["dve_done"], n)

            def setup():
                ve.memset(q[:, :, 0:TAPS - 1], 0.0)
                ve.memset(decay[0][:, :], 0.0)
                ve.memset(decay[1][:, :], 0.0).then_inc(s["pads_set"], 1)

            def setup_weights():
                dve.wait_ge(s["ld_conv"], LOADED_CONV)
                ts(conv_ws[:, :, :], conv_w[:, :, :], QS, None, ALU.mult).then_inc(s["taps_set"], 1)
                dve.wait_ge(s["wx_hi"], 1)
                tt(w_xr[:, :, :], w_x[:, :, :], w_x3[0][:, :, :], ALU.subtract).then_inc(s["wx_rest"], 1)
                dve.wait_ge(s["wx_mid"], 1)
                dve.wait_ge(s["wx_rest"], 1)
                tt(w_x3[2][:, :, :], w_xr[:, :, :], w_x3[1][:, :, :], ALU.subtract).then_inc(s["wx_lo"], 1)

            def setup_masks():
                dve.wait_ge(s["ld_att"], LOADED_ATT)
                for b in range(BATCH):
                    last = tt(masked[:, b, :, :], mask[:, :, :],
                              kmask[:, b:b + 1, :].to_broadcast([P, TT, T]), ALU.max)
                last.then_inc(s["masks_set"], 1)

            def norm_stats(src, st, mv, event):
                for a in range(TT):
                    last = ve.bn_stats(st[:, a, :], src[:, a, :])
                after(mark(last))
                for a in range(TT):
                    last = ve.bn_aggr(mv[:, a, :], st[:, a, :])
                last.then_inc(event, 1)

            def norm(dst, src, mv, rs):
                for a in range(TT):
                    last = ts(dst[:, a, :], src[:, a, :], mv[:, a, 0:1], rs[:, a:a + 1], ALU.subtract, ALU.mult)
                return last

            def f_stats(b):
                dve.wait_ge(ld_xt[b % XBUFS], 16 * (b // XBUFS + 1))
                norm_stats(x_t[b % XBUFS], f_st, f_mv, s["f_var"])

            def f_norm(b):
                dve.wait_ge(s["f_rstd"], b + 1)
                norm(xn, x_t[b % XBUFS], f_mv, f_rs).then_inc(s["f_xn"], 1)

            def f_quant(b, i):
                dve.wait_ge(s["f_xcopy"], 2 * b + i + 1)
                o = xq[:, 2 * i:2 * i + 2, :]
                after(mark(ts(o, o, 127.0, -128.0, ALU.min, ALU.max)))
                ts(q[:, 2 * i:2 * i + 2, TAPS - 1:TAPS - 1 + T], o, MAGIC, MAGIC, ALU.add,
                   ALU.subtract).then_inc(s["f_quant"], 1)

            def f_gate(b, i):
                dve.wait_ge(s["f_ztanh"], 2 * b + i + 1)
                if b >= 2:
                    dve.wait_ge(s["o_gated"], 2 * (b - 1))
                stt(out=zs[b % 2][:, 2 * i:2 * i + 2, :], in0=th[:, 2 * i:2 * i + 2, :], scalar=1.0,
                    in1=pair(f_ps), op0=ALU.add, op1=ALU.mult).then_inc(s["f_z"], 1)

            def f_conv(b, i):
                dve.wait_ge(s["f_tap"], 4 * b + 2 * i + 2)
                n = [0, 0]
                for tap in range(TAPS - 1):
                    for j in range(2):
                        c = 2 * i + j
                        if tap:
                            after(n[j])
                        ins = stt(out=v[:, c, :], in0=q[:, c, tap:tap + T], scalar=conv_ws[:, c, tap:tap + 1],
                                  in1=v[:, c, :], op0=ALU.mult, op1=ALU.add)
                        if tap < TAPS - 2:
                            n[j] = mark(ins)
                        else:
                            ins.then_inc(s["f_conv"], 1)

            def f_silu(b):
                dve.wait_ge(s["f_vtanh"], b + 1)
                return mark(stt(out=v[:, :, :], in0=th[:, :, :], scalar=1.0, in1=v[:, :, :],
                                op0=ALU.add, op1=ALU.mult))

            def f_uquant(b, n):
                after(n)
                after(mark(ts(v[:, :, :], v[:, :, :], 0.5 / QS, 127.0, ALU.mult, ALU.min)))
                ts(u[b % 2][:, :, :], v[:, :, :], MAGIC, MAGIC, ALU.add, ALU.subtract).then_inc(s["f_u"], 1)

            def f_split(b):
                dve.wait_ge(s["f_bhi"], b + 1)
                dve.wait_ge(s["f_dtin"], b + 1)
                tt(b_rest[:, :], pair(f_ps, 1), b_hi[b % 2][:, :], ALU.subtract).then_inc(s["f_brest"], 1)

            def f_split2(b):
                dve.wait_ge(s["f_bmid"], b + 1)
                tt(b_hi[b % 2][64:96, :], b_rest[64:96, :], b_mid[64:96, :], ALU.subtract).then_inc(s["f_bsplit"], 1)

            def f_pos(b, i):
                dve.wait_ge(s["f_dtproj"], 2 * b + i + 1)
                dve.wait_ge(s["f_abs"], 2 * b + i + 1)
                for j in range(2):
                    c = 2 * i + j
                    last = ts(dt_pos[:, c, :], pair(f_ps, j), dt_bias[:, c:c + 1], 0.0, ALU.add, ALU.max)
                last.then_inc(s["f_pos"], 1)

            def f_dt(b):
                dve.wait_ge(s["f_ln"], b + 1)
                dve.wait_ge(s["f_pos"], 2 * b + 2)
                tt(dt[b % 2][:, :, :], dt_pos[:, :, :], dt_abs[:, :, :], ALU.add).then_inc(s["f_dt"], 1)

            def f_dtu(b):
                dve.wait_ge(s["f_dt"], b + 1)
                stt(out=dtu[b % 2][:, :, :], in0=dt[b % 2][:, :, :], scalar=QS * QS, in1=u[b % 2][:, :, :],
                    op0=ALU.mult, op1=ALU.mult).then_inc(s["f_dtu"], 1)

            def scan(k):
                g, c = k // 4, k % 4
                dve.wait_ge(s["decay_ready"], k + 1)
                dve.wait_ge(s["bu_ready"], k + 1)
                if g >= 2:
                    dve.wait_ge(s["turned"], 4 * g - 4)
                ve.tensor_tensor_scan(h[:, g % 2, c, :, :].rearrange("p n t -> p (n t)"), decay[k % 2][:, :],
                                      bu[:, k % 3, :, :].rearrange("p n t -> p (n t)"), 0.0,
                                      ALU.mult, ALU.add).then_inc(s["scanned"], 1)

            def weigh(k):
                b, n, a = k // TICKS, 2 * ((k // 4) % NP) + (k // 2) % 2, k % 2
                dst, src, c = acc[b % 2][:, a, :], h_t[k % 2][:, :], c_t[b % 2][:, a, n:n + 1]
                dve.wait_ge(s["turned"], k + 1)
                dve.wait_ge(s["f_c"], b + 1)
                if n == 0:
                    if b >= 2:
                        dve.wait_ge(s["o_turned"], 2 * (b - 1))
                    ts(dst, src, c, None, ALU.mult).then_inc(s["weighted"], 1)
                else:
                    dve.wait_ge(s["weighted"], k - 1)
                    stt(out=dst, in0=src, scalar=c, in1=dst, op0=ALU.mult, op1=ALU.add).then_inc(s["weighted"], 1)

            def o_skip(b, i):
                dve.wait_ge(s["o_turned"], 2 * b + i + 1)
                for j in range(2):
                    c = 2 * i + j
                    last = stt(out=yd[:, c, :], in0=u[b % 2][:, c, :], scalar=d_skip[:, c:c + 1],
                               in1=pair(r_ps[i], j), op0=ALU.mult, op1=ALU.add)
                last.then_inc(s["o_skip"], 1)

            def o_x1(b):
                dve.wait_ge(s["o_mm"], b + 1)
                tt(x1[:, :, :], pair(r_ps[0]), x_t[b % XBUFS][:, :, :], ALU.add).then_inc(s["o_x1"], 1)

            def a_stats(b):
                dve.wait_ge(s["o_x1"], b + 1)
                norm_stats(x1, a_st, a_mv, s["a_var"])

            def a_gate(b):
                dve.wait_ge(s["a_rstd"], b + 1)
                dve.wait_ge(s["a_sc"], b + 1)
                n = mark(norm(qc, x1, a_mv, a_rs))
                after(n)
                return mark(tt(sc[:, :, :], sc[:, :, :], qc[:, :, :], ALU.mult))

            def a_mask(b, n):
                after(n)
                dve.wait_ge(s["masks_set"], 1)
                after(mark(stt(out=sc[:, :, :], in0=masked[:, b, :, :], scalar=MASKED, in1=sc[:, :, :],
                               op0=ALU.mult, op1=ALU.add)))
                after(mark(ve.tensor_reduce(a_mx[:, :], sc[:, :, :], AX.X, ALU.max)))
                ts(a_nm[:, :], a_mx[:, :], -1.0, None, ALU.mult).then_inc(s["a_max"], 1)

            def a_x2(b):
                dve.wait_ge(s["a_exp"], b + 1)
                after(mark(ve.reciprocal(a_rec[:, :], a_sum[:, :])))
                for a in range(TT):
                    last = stt(out=x2[:, a, :], in0=sc[:, a, :], scalar=a_rec[:, a:a + 1], in1=x1[:, a, :],
                               op0=ALU.mult, op1=ALU.add)
                last.then_inc(s["a_x2"], 1)
                dve.wait_ge(s["a_x2"], b + 1)
                norm_stats(x2, n_st, n_mv, s["n_var"])

            def n_norm(b):
                dve.wait_ge(s["n_rstd"], b + 1)
                norm(xf, x2, n_mv, n_rs).then_inc(s["n_xf"], 1)

            def g_top(b):
                dve.wait_ge(s["g_mm"], b + 1)
                after(mark(ve.tensor_copy(lg[:, :, :], r_ps[0][:, 0:TT * E].rearrange("p (a e) -> p a e", a=TT))))
                for a in range(TT):
                    last = ve.max(out=top[:, a, :], in_=lg[:, a, :])
                after(mark(last))
                tt(g_d[:, :], top[:, :, 1], top[:, :, 0], ALU.subtract).then_inc(s["g_diff"], 1)
                for a in range(TT):
                    last = ve.max_index(out=topi[:, a, :], in_max=top[:, a, :], in_values=lg[:, a, :])
                after(mark(last))
                after(mark(ve.tensor_copy(topf[:, :, :], topi[:, :, :])))
                for i in range(2):
                    for a in range(TT):
                        last = ts(hot[:, i, a, :], rank_expert[:, :], topf[:, a, i:i + 1], None, ALU.is_equal)
                last.then_inc(s["g_hot"], 1)

            def g_weights(b):
                dve.wait_ge(s["g_exp"], b + 1)
                after(mark(ts(g_one[:, :], g_ex[:, :], 1.0, None, ALU.add)))
                after(mark(ve.reciprocal(g_rec[:, :], g_one[:, :])))
                ts(g_w[:, 0, :], g_rec[:, :], 0.5, None, ALU.mult)
                stt(out=g_w[:, 1, :], in0=g_rec[:, :], scalar=0.5, in1=g_ex[:, :], op0=ALU.mult,
                    op1=ALU.mult).then_inc(s["g_wts"], 1)

            def g_select(b):
                dve.wait_ge(s["g_hcopy"], b + 1)
                dve.wait_ge(s["g_xa"], b + 1)
                n = mark(tt(hot_d, hot_t[:, 1, :], hot_t[:, 0, :], ALU.subtract))
                for o in range(2):
                    last = stt(out=xa1[:, o, :], in0=pair(r_ps[1], o), scalar=2.0, in1=hot_t[:, 0, :],
                               op0=ALU.mult, op1=ALU.mult)
                last.then_inc(s["g_xa1"], 1)
                after(n)
                for o in range(2):
                    last = stt(out=xad[:, o, :], in0=pair(r_ps[1], o), scalar=2.0, in1=hot_d,
                               op0=ALU.mult, op1=ALU.mult)
                last.then_inc(s["g_xad"], 1)

            def ffn_gate(b, j):
                f, n = 2 * (j // 4) + j % 2, 12 * b
                dve.wait_ge(s["h_tanh"], n + j + 1)
                dve.wait_ge(s["h_copy"], n + j + 1)
                if n + j >= 2:
                    dve.wait_ge(s["h_act"], n + j - 1)
                stt(out=hg[:, j % 2, :], in0=ht[:, j % 2, :], scalar=1.0, in1=pair(r_ps[(f + 1) % 2], 0),
                    op0=ALU.add, op1=ALU.mult).then_inc(s["h_gate"], 1)

            def p_mask(b):
                dve.wait_ge(s["p_mm"], b + 1)
                stt(out=p_m[:, :, :], in0=pair(r_ps[1]), scalar=2.0, in1=hot_t[:, :, :], op0=ALU.mult,
                    op1=ALU.mult).then_inc(s["p_mask"], 1)

            def e_out(b):
                dve.wait_ge(s["e_mm"], b + 1)
                if b:
                    dve.wait_ge(s["stored"], 16 * b)
                tt(xo[:, :, :], pair(r_ps[0]), x2[:, :, :], ALU.add).then_inc(s["e_done"], 1)

            setup()
            pending = 0
            for slot in SLOTS:
                f, r = front_at(slot), rest_at(slot)
                for k in range(TICKS):
                    tick = slot * TICKS + k
                    if (st := step(tick, 0)) is not None:
                        scan(st)
                    if (st := step(tick, CLAG)) is not None:
                        weigh(st)
                    if f is not None:
                        if k == 0:
                            f_stats(f)
                        if k == 1:
                            f_norm(f)
                        if slot == -1 and k == 2:
                            setup_weights()
                        if slot == -1 and k == 22:
                            setup_masks()
                        if 4 <= k < 6:
                            f_quant(f, k - 4)
                        if k == 8:
                            f_conv(f, 0)
                        if k == 10:
                            f_conv(f, 1)
                        if 11 <= k < 13:
                            f_gate(f, k - 11)
                        if k == 13:
                            pending = f_silu(f)
                        if k == 14:
                            f_uquant(f, pending)
                        if k == 16:
                            f_split(f)
                        if k == 18:
                            f_split2(f)
                        if 19 <= k < 21:
                            f_pos(f, k - 19)
                        if k == 23:
                            f_dt(f)
                            f_dtu(f)
                    if r is not None:
                        if 7 <= k < 9:
                            o_skip(r, k - 7)
                        if k == 9:
                            o_x1(r)
                            a_stats(r)
                        if k == 11:
                            pend_a = a_gate(r)
                        if k == 12:
                            a_mask(r, pend_a)
                        if k == 13:
                            a_x2(r)
                        if k == 14:
                            n_norm(r)
                        if k == 17:
                            g_top(r)
                            g_weights(r)
                        if k == 18:
                            g_select(r)
                        if 19 <= k < 31:
                            ffn_gate(r, k - 19)
                        if k == 31:
                            p_mask(r)
                            e_out(r)


def kernel(**inputs):
    import numpy as np
    import ml_dtypes
    import concourse.bacc as bacc
    from concourse.bass_utils import run_bass_kernel_spmd

    a = {k: np.asarray(v) for k, v in inputs.items()}

    def rows(w):
        return w.reshape(-1, P, w.shape[-1]).transpose(1, 0, 2)

    def col(vec):
        return vec.reshape(-1, P).T

    def pad(w, axis):
        widths = [(0, 0)] * w.ndim
        widths[axis] = (0, FT * P - FF)
        return np.pad(w, widths)

    w_x = a["L0_attn_W_x"].T
    wide = np.zeros((DI, 2 * P + NS), w_x.dtype)
    wide[:, 0:P] = w_x[:, 0:P]
    for i in range(3):
        wide[:, P + 32 * i:P + 32 * i + NS] = w_x[:, P:P + NS]
    wide[:, 2 * P:] = w_x[:, P + NS:]

    ident = np.eye(P, dtype=np.float32)
    had = np.ones((1, 1), np.float32)
    while had.shape[0] < P:
        had = np.block([[had, had], [had, -had]])
    sel = np.zeros((P, NS, P), ml_dtypes.bfloat16)
    for n in range(NS):
        for i in range(3):
            sel[32 * i + n, n, :] = 1
    rank_expert = np.repeat(np.arange(E, dtype=np.float32), R)[None, :].repeat(P, 0)

    arrays = {
        "x": a["x"],
        "ident": ident, "identb": ident.astype(ml_dtypes.bfloat16), "had": had, "sel": sel,
        "rank_expert": rank_expert,
        "w_in": rows(a["L0_attn_W_in"].T),
        "conv_w": a["L0_attn_conv_w"].reshape(CT, P, TAPS).transpose(1, 0, 2),
        "conv_b": col(a["L0_attn_conv_b"]),
        "w_x": rows(wide),
        "w_dt": a["L0_attn_W_dt"].T,
        "dt_bias": col(a["L0_attn_dt_bias"]),
        "a_log": a["L0_attn_A"].reshape(CT, P, NS).transpose(1, 0, 2),
        "d_skip": col(a["L0_attn_D"]),
        "w_out": rows(a["L0_attn_W_out"].T),
        "ctx_t": a["ctx_512"].transpose(2, 0, 1),
        "w_q": a["L0_xattn_Wq"].T, "w_k": a["L0_xattn_Wk"].T,
        "b_qk": np.stack([a["L0_xattn_bq"], a["L0_xattn_bk"]], 1),
        "mask": a["mask_SxS2_bk1"].reshape(TT, P, T).transpose(1, 0, 2),
        "kmask": np.broadcast_to(a["mask_BxS2_bf0"][None], (P, BATCH, T)),
        "gate": rows(a["L0_ffn_gate_w"].T),
        "w1": rows(pad(a["L0_ffn_w1"], 0).T), "w3": rows(pad(a["L0_ffn_w3"], 0).T),
        "w2": rows(pad(a["L0_ffn_w2"], 1).T),
        "la1": rows(a["L0_ffn_a1"].reshape(E * R, D).T), "la3": rows(a["L0_ffn_a3"].reshape(E * R, D).T),
        "lb1": pad(a["L0_ffn_b1"], 1).transpose(0, 2, 1).reshape(E * R, FT * P),
        "lb3": pad(a["L0_ffn_b3"], 1).transpose(0, 2, 1).reshape(E * R, FT * P),
        "la2": rows(pad(a["L0_ffn_a2"], 2).reshape(E * R, FT * P).T),
        "lb2": a["L0_ffn_b2"].transpose(0, 2, 1).reshape(E * R, D),
    }
    arrays = {f"in_{k}": np.ascontiguousarray(v) for k, v in arrays.items()}
    nc = bacc.Bacc("TRN2", target_bir_lowering=False, num_devices=1)
    t = {k[3:]: nc.dram_tensor(k, v.shape, mybir.dt.from_np(v.dtype), kind="ExternalInput").ap()
         for k, v in arrays.items()}
    t["out"] = nc.dram_tensor("out_0", (BATCH, T, D), F32, kind="ExternalOutput").ap()
    build(nc, t)
    r = run_bass_kernel_spmd(nc, [arrays], core_ids=[0])
    return r.results[0]["out_0"]
```

```python
from contextlib import ExitStack

import concourse.bass as bass
from concourse import mybir

F32 = mybir.dt.float32
BF16 = mybir.dt.bfloat16
U8 = mybir.dt.uint8
U32 = mybir.dt.uint32
ALU = mybir.AluOpType
ACT = mybir.ActivationFunctionType
AX = mybir.AxisListType

P = 128
BATCH, T, D = 4, 256, 256
TT = T // P
DK = D // P
DI = 512
CT = DI // P
NS = 16
NP = NS // 2
TAPS = 4
RANK = P
H = 64
E, R = 8, 16
FF = 704
FT = -(-FF // P)
EPS = 1e-5
QS = 0.05
MAGIC = 1.5 * 2.0 ** 23
MASKED = -1e30

TICKS = CT * NP
AHEAD = 1
BAHEAD = 6
XBUFS = 3
HRING = 3
BRING = 3
TLAG = 5
CLAG = 7
FIRST = -TICKS
LAST = (BATCH + 1) * TICKS + 21


def build(nc, t):
    with ExitStack() as ctx:
        def sb(name, shape, dt=F32):
            return ctx.enter_context(nc.sbuf_tensor(name, shape, dt))

        def psum(name):
            return ctx.enter_context(nc.psum_tensor(name, [P, 512], F32))

        def sems(names):
            return {n: ctx.enter_context(nc.semaphore(n)) for n in names.split()}

        ident = sb("ident", [P, P])
        identb = sb("identb", [P, P], BF16)
        had = sb("had", [P, P])
        sel = sb("sel", [P, NS], BF16)
        rank_expert = sb("rank_expert", [P, P])
        w_in = sb("w_in", [P, DK, 2 * DI])
        conv_w = sb("conv_w", [P, CT, TAPS])
        conv_ws = sb("conv_ws", [P, CT, TAPS])
        conv_b = sb("conv_b", [P, CT])
        WX = 2 * P + NS
        w_x3 = [sb(f"w_x3_{i}", [P, CT, WX], BF16) for i in range(3)]
        w_dt = sb("w_dt", [P, DI])
        dt_bias = sb("dt_bias", [P, CT])
        a_log = sb("a_log", [P, CT, NS])
        d_skip = sb("d_skip", [P, CT])
        w_oh = sb("w_oh", [P, CT, D])
        ctx_t = sb("ctx_t", [H, BATCH, T])
        w_q = sb("w_q", [H, H])
        w_k = sb("w_k", [H, H])
        b_qk = sb("b_qk", [H, 2])
        masked = sb("masked", [P, BATCH, TT, T], U8)
        gate = sb("gate", [P, DK, E])
        w1 = sb("w1", [P, DK, FT * P])
        w3 = sb("w3", [P, DK, FT * P])
        w2 = sb("w2", [P, FT, D])
        la1 = sb("la1", [P, DK, P])
        la3 = sb("la3", [P, DK, P])
        lb1 = sb("lb1", [P, FT * P])
        lb3 = sb("lb3", [P, FT * P])
        la2 = sb("la2", [P, FT, P])
        lb2 = sb("lb2", [P, D])

        minus_half = sb("minus_half", [P, TT])

        x_t = [sb(f"x_t{i}", [P, TT, D]) for i in range(XBUFS)]
        f_st = sb("f_st", [P, TT, 6])
        f_mv = sb("f_mv", [P, TT, 2])
        f_rs = sb("f_rs", [P, TT])
        xn = sb("xn", [P, TT, D])
        xn_t = sb("xn_t", [P, DK, T])
        q = sb("q", [P, CT, TAPS - 1 + T], BF16)
        v = sb("v", [P, CT, T])
        zs = [sb(f"zs{i}", [P, CT, T]) for i in range(2)]
        u = [sb(f"u{i}", [P, CT, T], BF16) for i in range(2)]
        dt_in = sb("dt_in", [P, T])
        b_hi = [sb(f"b_hi{i}", [P, T], BF16) for i in range(2)]
        b_rest = sb("b_rest", [P, T])
        b_mid = sb("b_mid", [P, T], BF16)
        c_t = [sb(f"c_t{i}", [P, TT, NS]) for i in range(2)]
        dt_abs = sb("dt_abs", [P, CT, T])
        xq = th = dt_abs
        dt_pos = v
        dt = [sb(f"dt{i}", [P, CT, T]) for i in range(2)]
        dtu = [sb(f"dtu{i}", [P, CT, T]) for i in range(2)]

        b_rep = sb("b_rep", [P, BRING, 2, T])
        bu = sb("bu", [P, 3, 2, T])
        h = sb("h", [P, HRING, CT, 2, T])
        acc = [sb(f"acc{i}", [P, TT, DI]) for i in range(2)]

        yd = sb("yd", [P, CT, T])
        x1 = sb("x1", [P, TT, D])
        qk = sb("qk", [H, 2, T])
        sc = sb("sc", [P, TT, T])
        a_st = sb("a_st", [P, TT, 6])
        a_mv = sb("a_mv", [P, TT, 2])
        a_rs = sb("a_rs", [P, TT])
        a_mx = sb("a_mx", [P, TT])
        a_nm = sb("a_nm", [P, TT])
        a_sum = sb("a_sum", [P, TT])
        a_rec = sb("a_rec", [P, TT])
        x2 = [sb(f"x2_{i}", [P, TT, D]) for i in range(2)]
        n_st = sb("n_st", [P, TT, 6])
        n_mv = sb("n_mv", [P, TT, 2])
        n_rs = sb("n_rs", [P, TT])
        xf = sb("xf", [P, TT, D])
        qc = xf
        xf_t = sb("xf_t", [P, DK, T])
        lg = sb("lg", [P, TT, E])
        top = sb("top", [P, TT, 8])
        topi = sb("topi", [P, TT, 8], U32)
        topf = sb("topf", [P, TT, 8])
        g_d = sb("g_d", [P, TT])
        g_ex = sb("g_ex", [P, TT])
        g_one = sb("g_one", [P, TT])
        g_rec = sb("g_rec", [P, TT])
        g_w = sb("g_w", [P, 2, TT])
        hot = sb("hot", [P, 2, TT, P], BF16)
        hot_t = sb("hot_t", [P, 2, T])
        w_rep = sb("w_rep", [P, 2, T])
        xa1 = sb("xa1", [P, 2, T])
        xad = sb("xad", [P, 2, T])
        ht = sb("ht", [P, 2, T])
        h3 = sb("h3", [P, 2, T])
        hot_d = h3[:, 0, :]
        hg = sb("hg", [P, 2, T])
        aw = sb("aw", [P, FT, 2, T])
        aws = sb("aws", [P, FT, T])
        p_m = xa1
        p_s = ht[:, 0, :]
        w_x, w_xr = (h[:, i, :, :, :].rearrange("p c n t -> p (c n t)")[:, 0:CT * WX].rearrange(
            "p (c n) -> p c n", c=CT) for i in range(2))
        mask = aws[:, 0:1, 0:TT * T // 4].bitcast(U8).rearrange("p o (a t) -> p (o a) t", a=TT)
        kmask = aws[:, 1:2, 0:BATCH * T // 4].bitcast(U8).rearrange("p o (b t) -> p (o b) t", b=BATCH)
        w_out, w_bf = (aw[:, 2 * i:2 * i + 2, :, :].rearrange("p f i t -> p (f i) t") for i in range(2))

        decay = [psum(f"decay{i}") for i in range(2)]
        h_t = [psum(f"h_t{i}") for i in range(2)]
        work = [psum(f"work{i}") for i in range(4)]
        f_ps, r_ps, ffn_ps = work[0], work[1], work[2:4]

        s = sems(
            "ld_x0 ld_x1 ld_x2 ld_id ld_in ld_conv ld_x ld_sel ld_out ld_att ld_ffn stored "
            "half_set eps_added pads_set taps_set wx_hi wx_rest wx_mid wx_lo had_sum had_mm had_done masks_set "
            "f_var f_rstd f_xn f_turned f_xn_t f_projx f_projz f_xcopy f_quant f_tap f_conv f_ztanh f_z "
            "f_vtanh f_silu f_u f_xproj f_cproj f_dtin f_bhi f_brest f_bmid f_bsplit f_c f_dtproj "
            "f_abs f_pos f_exp f_ln f_dt f_dtu "
            "b_spread b_copied bu_ready decay_ready scanned turned weighted "
            "o_turned o_skip o_gated o_mm o_x1 a_qkmm a_qk a_scmm a_sc a_var a_rstd a_gated a_max a_exp a_x2 "
            "n_var n_rstd n_xf n_turned n_xft g_mm g_lg g_xa g_diff g_exp g_wts g_hot g_hturned g_hcopy "
            "g_wturned g_wcopy g_xa1 g_xad h_mm h_tanh h_copy h_gate h_pair h_act h_sum p_mm p_mask "
            "p_sum e_mm e_done "
            "dve_done")
        ld_xt = [s["ld_x0"], s["ld_x1"], s["ld_x2"]]

        def pair(bank, i=None):
            v2 = bank[:, :].rearrange("p (a t) -> p a t", a=2)
            return v2 if i is None else v2[:, i, :]

        def step(tick, offset):
            k = tick - offset
            return k if 0 <= k < BATCH * TICKS else None

        def ffn_half(j):
            return 2 * (j // 4) + j % 2, (j // 2) % 2

        def fronts(tick):
            return [(b, tick - TICKS * (b - 1)) for b in range(BATCH) if 0 <= tick - TICKS * (b - 1) < TICKS]

        def rests(tick):
            return [(b, tick - TICKS * (b + 1)) for b in range(BATCH) if 0 <= tick - TICKS * (b + 1) < 2 * TICKS]

        def ffn_age(j):
            return 31 + 5 * j // 4

        block = ctx.enter_context(nc.Block())

        @block.sync
        def _(sp):
            def x_load(b):
                sp.dma_start(x_t[b % XBUFS][:, :, :],
                             t["x"][b].rearrange("(a p) d -> p a d", p=P)).then_inc(ld_xt[b % XBUFS], 16)

            x_load(0)
            sp.dma_start(ident[:, :], t["ident"]).then_inc(s["ld_id"], 16)
            sp.dma_start(w_in[:, :, :], t["w_in"]).then_inc(s["ld_in"], 16)
            for dst, name in ((conv_w[:, :, :], "conv_w"), (conv_b[:, :], "conv_b"), (d_skip[:, :], "d_skip"),
                              (a_log[:, :, :], "a_log"), (dt_bias[:, :], "dt_bias")):
                sp.dma_start(dst, t[name]).then_inc(s["ld_conv"], 16)
            sp.dma_start(w_x[:, :, :], t["w_x"]).then_inc(s["ld_x"], 16)
            sp.dma_start(w_dt[:, :], t["w_dt"]).then_inc(s["ld_x"], 16)
            sp.dma_start(sel[:, :], t["sel"]).then_inc(s["ld_sel"], 16)
            sp.dma_start(w_out[:, :, :], t["w_out"]).then_inc(s["ld_out"], 16)
            sp.dma_start(had[:, :], t["had"]).then_inc(s["ld_out"], 16)
            x_load(1)
            x_load(2)
            for dst, name in ((ctx_t[:, :, :], "ctx_t"), (w_q[:, :], "w_q"), (w_k[:, :], "w_k"),
                              (b_qk[:, :], "b_qk"), (mask[:, :, :], "mask"), (kmask[:, :, :], "kmask")):
                sp.dma_start(dst, t[name]).then_inc(s["ld_att"], 16)
            for dst, name in ((gate[:, :, :], "gate"), (la1[:, :, :], "la1"), (la3[:, :, :], "la3"),
                              (rank_expert[:, :], "rank_expert"), (identb[:, :], "identb"),
                              (w1[:, :, :], "w1"), (w3[:, :, :], "w3"), (lb1[:, :], "lb1"), (lb3[:, :], "lb3"),
                              (w2[:, :, :], "w2"), (la2[:, :, :], "la2"), (lb2[:, :], "lb2")):
                sp.dma_start(dst, t[name]).then_inc(s["ld_ffn"], 16)
            for b in range(BATCH):
                if b + XBUFS < BATCH:
                    sp.wait_ge(s["o_x1"], b + 1)
                    x_load(b + XBUFS)
                sp.wait_ge(s["e_done"], b + 1)
                sp.dma_start(t["out"][b].rearrange("(a p) d -> p a d", p=P),
                             x2[b % 2][:, :, :]).then_inc(s["stored"], 16)
            sp.wait_ge(s["stored"], 16 * BATCH)

        LOADED_CONV, LOADED_X, LOADED_OUT, LOADED_ATT, LOADED_FFN = 5 * 16, 2 * 16, 2 * 16, 6 * 16, 12 * 16

        @block.tensor
        def _(pe):
            mm, turn = nc.tensor.matmul, nc.tensor.transpose

            readers = {}

            def take(bank, *events):
                for event, count in readers.get(id(bank), ()):
                    pe.wait_ge(s[event], count)
                readers[id(bank)] = events

            def hadamard_out():
                pe.wait_ge(s["ld_out"], LOADED_OUT)
                pe.wait_ge(s["had_sum"], 4)
                for i in range(2):
                    take(ffn_ps[i], ("had_done", i + 1))
                    for j in range(2):
                        last = mm(pair(ffn_ps[i], j), had[:, :], w_bf[:, 2 * i + j, :], start=True, stop=True)
                    last.then_inc(s["had_mm"], 1)

            def f_turn(b):
                pe.wait_ge(s["ld_id"], 16)
                pe.wait_ge(s["f_xn"], b + 1)
                take(f_ps, ("f_xn_t", b + 1))
                for k in range(DK):
                    for a in range(TT):
                        last = turn(pair(f_ps, k)[:, a * P:a * P + P], xn[:, a, k * P:k * P + P], ident[:, :])
                last.then_inc(s["f_turned"], 1)

            def project(bank, b, i):
                pe.wait_ge(s["ld_in"], 16)
                pe.wait_ge(s["f_xn_t"], b + 1)
                for j in range(2):
                    c = 2 * i + j
                    for k in range(DK):
                        last = mm(pair(bank, j), w_in[:, k, c * P:c * P + P], xn_t[:, k, :],
                                  start=(k == 0), stop=(k == DK - 1))
                return last

            def f_proj_x(b, i):
                take(f_ps, ("f_xcopy", 2 * b + i + 1))
                project(f_ps, b, i).then_inc(s["f_projx"], 1)

            def f_proj_z(b, i):
                bank = (f_ps, r_ps)[i]
                take(bank, ("f_ztanh", 2 * b + i + 1), ("f_z", 2 * b + i + 1))
                project(bank, b, 2 + i).then_inc(s["f_projz"], 1)

            def f_xproj(b):
                pe.wait_ge(s["wx_lo"], 1)
                pe.wait_ge(s["f_u"], b + 1)
                take(f_ps, ("f_dtin", b + 1), ("f_bhi", b + 1), ("f_brest", b + 1))
                for j in range(2):
                    n = 0
                    for k in range(CT):
                        for part in w_x3:
                            last = mm(pair(f_ps, j), part[:, k, j * P:j * P + P], u[b % 2][:, k, :],
                                      start=(n == 0), stop=(n == 3 * CT - 1))
                            n += 1
                last.then_inc(s["f_xproj"], 1)

            def f_cproj(b):
                take(f_ps, ("f_c", b + 1))
                for a in range(TT):
                    n = 0
                    for k in range(CT):
                        for part in w_x3:
                            last = mm(f_ps[:, a * NS:a * NS + NS], u[b % 2][:, k, a * P:a * P + P],
                                      part[:, k, 2 * P:2 * P + NS], start=(n == 0), stop=(n == 3 * CT - 1))
                            n += 1
                last.then_inc(s["f_cproj"], 1)

            def f_dtproj(b, i):
                pe.wait_ge(s["ld_x"], LOADED_X)
                pe.wait_ge(s["f_dtin"], b + 1)
                take(f_ps, ("f_abs", 2 * b + i + 1), ("f_pos", 2 * b + i + 1))
                for j in range(2):
                    c = 2 * i + j
                    last = mm(pair(f_ps, j), w_dt[:, c * P:c * P + P], dt_in[:, :], start=True, stop=True)
                last.then_inc(s["f_dtproj"], 1)

            def spread_b(g):
                b, n = g // NP, g % NP
                pe.wait_ge(s["ld_sel"], 16)
                pe.wait_ge(s["f_bsplit"], b + 1)
                take(r_ps, ("b_copied", g + 1))
                for j in range(2):
                    last = mm(pair(r_ps, j), sel[:, 2 * n + j:2 * n + j + 1].to_broadcast([P, P]), b_hi[b % 2][:, :], start=True, stop=True)
                last.then_inc(s["b_spread"], 1)

            def turn_h(k):
                g, n, a = k // 4, (k // 2) % 2, k % 2
                pe.wait_ge(s["scanned"], 4 * g + 4)
                take(h_t[k % 2], ("weighted", k + 1))
                for c in range(CT):
                    last = turn(h_t[k % 2][:, c * P:c * P + P], h[:, g % HRING, c, n, a * P:a * P + P], ident[:, :])
                last.then_inc(s["turned"], 1)

            def a_qk(b):
                pe.wait_ge(s["ld_att"], LOADED_ATT)
                take(r_ps, ("a_qk", 2 * b + 2))
                for i, w in enumerate((w_q, w_k)):
                    last = mm(pair(r_ps, i)[0:H, :], w[:, :], ctx_t[:, b, :], start=True, stop=True)
                last.then_inc(s["a_qkmm"], 1)

            def a_scores(b):
                pe.wait_ge(s["a_qk"], 2 * b + 2)
                take(r_ps, ("a_sc", b + 1))
                for a in range(TT):
                    last = mm(pair(r_ps, a), qk[:, 0, a * P:a * P + P], qk[:, 1, :], start=True, stop=True)
                last.then_inc(s["a_scmm"], 1)

            def o_turn(b, i):
                pe.wait_ge(s["weighted"], TICKS * (b + 1))
                take(r_ps, ("o_skip", 2 * b + i + 1))
                for j in range(2):
                    for a in range(TT):
                        c = 2 * i + j
                        last = turn(pair(r_ps, j)[:, a * P:a * P + P],
                                    acc[b % 2][:, a, c * P:c * P + P], ident[:, :])
                last.then_inc(s["o_turned"], 1)

            def o_proj(b, a):
                pe.wait_ge(s["o_gated"], 2 * b + 2)
                if a == 0:
                    pe.wait_ge(s["had_done"], 2)
                    take(r_ps, ("o_x1", b + 1))
                for c in range(CT):
                    last = mm(pair(r_ps, a), yd[:, c, a * P:a * P + P], w_oh[:, c, :],
                              start=(c == 0), stop=(c == CT - 1))
                last.then_inc(s["o_mm"], 1)

            def n_turn(b):
                pe.wait_ge(s["n_xf"], b + 1)
                take(r_ps, ("n_xft", b + 1))
                for k in range(DK):
                    for a in range(TT):
                        last = turn(pair(r_ps, k)[:, a * P:a * P + P], xf[:, a, k * P:k * P + P], ident[:, :])
                last.then_inc(s["n_turned"], 1)

            def g_logits(b):
                pe.wait_ge(s["ld_ffn"], LOADED_FFN)
                pe.wait_ge(s["n_xft"], b + 1)
                take(r_ps, ("g_lg", b + 1))
                for a in range(TT):
                    for k in range(DK):
                        last = mm(r_ps[:, a * E:a * E + E], xf_t[:, k, a * P:a * P + P], gate[:, k, :],
                                  start=(k == 0), stop=(k == DK - 1))
                last.then_inc(s["g_mm"], 1)

            def g_lora(b):
                take(r_ps, ("g_xa1", b + 1), ("g_xad", b + 1))
                for i, w in enumerate((la1, la3)):
                    for k in range(DK):
                        last = mm(pair(r_ps, i), w[:, k, :], xf_t[:, k, :], start=(k == 0), stop=(k == DK - 1))
                last.then_inc(s["g_xa"], 1)

            def g_turn_hot(b):
                pe.wait_ge(s["g_hot"], b + 1)
                take(f_ps, ("g_hcopy", b + 1))
                hb = f_ps[:, 0:256].bitcast(BF16).rearrange("p (s t) -> p s t", s=2)
                for i in range(2):
                    for a in range(TT):
                        last = turn(hb[:, i, a * P:a * P + P], hot[:, i, a, :], identb[:, :])
                last.then_inc(s["g_hturned"], 1)

            def g_turn_w(b):
                pe.wait_ge(s["g_wts"], b + 1)
                take(f_ps, ("g_wcopy", b + 1))
                for i in range(2):
                    for a in range(TT):
                        last = turn(pair(f_ps, i)[:, a * P:a * P + P],
                                    g_w[:, i, a:a + 1].to_broadcast([P, P]), ident[:, :])
                last.then_inc(s["g_wturned"], 1)

            def ffn_up(b, j):
                f, i = ffn_half(j)
                bank, n = ffn_ps[f % 2], 2 * FT * b + j + 1
                if i == 0:
                    pe.wait_ge(s["g_xa1"], b + 1)
                else:
                    pe.wait_ge(s["g_xad"], b + 1)
                take(bank, ("h_copy", n), ("h_gate", n))
                for o, (w, lb) in enumerate(((w1, lb1), (w3, lb3))):
                    if i == 0:
                        for k in range(DK):
                            mm(pair(bank, o), w[:, k, f * P:f * P + P], xf_t[:, k, :],
                               start=(k == 0 and o == 0), stop=False, skip_group_check=True)
                    last = mm(pair(bank, o), lb[:, f * P:f * P + P], (xad if i else xa1)[:, o, :],
                              start=False, stop=True, skip_group_check=True)
                last.then_inc(s["h_mm"], 1)

            def ffn_ranks(b, part):
                if part == 0:
                    take(ffn_ps[0], ("p_mask", b + 1))
                for f in range(2 * part, 2 * part + 2):
                    pe.wait_ge(s["h_act"], 2 * FT * b + 4 * (f // 2) + f % 2 + 3)
                    last = mm(ffn_ps[0][:, :], la2[:, f, :], aw[:, f, :, :], start=(f == 0), stop=(f == FT - 1))
                if part == FT // 2 - 1:
                    last.then_inc(s["p_mm"], 1)

            def ffn_down(b, part):
                a, half = part // 2, part % 2
                if part == 0:
                    take(ffn_ps[1], ("e_done", b + 1))
                pe.wait_ge(s["h_sum"], FT * b + 3 * half + 3)
                for f in range(3 * half, 3 * half + 3):
                    mm(pair(ffn_ps[1], a), aws[:, f, a * P:a * P + P], w2[:, f, :],
                       start=(part == 0 and f == 0), stop=False, skip_group_check=True)

            def ffn_down_lora(b):
                pe.wait_ge(s["p_sum"], b + 1)
                for a in range(TT):
                    last = mm(pair(ffn_ps[1], a), p_s[:, a * P:a * P + P], lb2[:, :],
                              start=False, stop=True, skip_group_check=True)
                last.then_inc(s["e_mm"], 1)

            def front(b, age):
                if age == 3:
                    f_turn(b)
                if age in (5, 7):
                    f_proj_x(b, (age - 5) // 2)
                if age in (13, 16):
                    f_proj_z(b, (age - 13) // 3)
                if age == 17:
                    f_xproj(b)
                if age == 20:
                    f_cproj(b)
                if age in (22, 24):
                    f_dtproj(b, (age - 22) // 2)

            def rest(b, age):
                if age == 2:
                    a_qk(b)
                if age == 4:
                    a_scores(b)
                if age in (7, 9):
                    o_turn(b, (age - 7) // 2)
                if age in (12, 13):
                    o_proj(b, age - 12)
                if age == 22:
                    n_turn(b)
                if age == 24:
                    g_logits(b)
                if age == 26:
                    g_lora(b)
                if age == 28:
                    g_turn_hot(b)
                if age == 29:
                    g_turn_w(b)
                for j in range(2 * FT):
                    if age == ffn_age(j):
                        ffn_up(b, j)
                if 47 <= age < 50:
                    ffn_ranks(b, age - 47)
                if 47 <= age < 51:
                    ffn_down(b, age - 47)
                if age == 51:
                    ffn_down_lora(b)

            for tick in range(FIRST, LAST):
                if (st := step(tick, TLAG)) is not None:
                    turn_h(st)
                if (st := step(tick, -BAHEAD)) is not None and st % 4 == 0:
                    spread_b(st // 4)
                for b, age in rests(tick):
                    rest(b, age)
                for b, age in fronts(tick):
                    front(b, age)
                if tick == FIRST + 22:
                    hadamard_out()

        @block.scalar
        def _(act):
            go = nc.scalar.activation

            def split_wx():
                act.wait_ge(s["ld_x"], LOADED_X)
                go(w_x3[0][:, :, :], w_x[:, :, :], ACT.Copy).then_inc(s["wx_hi"], 1)
                act.wait_ge(s["wx_rest"], 1)
                go(w_x3[1][:, :, :], w_xr[:, :, :], ACT.Copy).then_inc(s["wx_mid"], 1)

            def hadamard_out():
                for i in range(2):
                    act.wait_ge(s["had_mm"], i + 1)
                    go(w_oh[:, 2 * i:2 * i + 2, :], pair(ffn_ps[i]), ACT.Copy,
                       scale=DI ** -0.5 * QS * 0.5).then_inc(s["had_done"], 1)

            def f_xn_copy(b):
                act.wait_ge(s["f_turned"], b + 1)
                go(xn_t[:, :, :], pair(f_ps), ACT.Copy).then_inc(s["f_xn_t"], 1)

            def f_xcopy(b, i):
                act.wait_ge(s["f_projx"], 2 * b + i + 1)
                if b:
                    act.wait_ge(s["f_dt"], b)
                go(xq[:, 2 * i:2 * i + 2, :], pair(f_ps), ACT.Copy, scale=1.0 / QS).then_inc(s["f_xcopy"], 1)

            def f_ztanh(b, i):
                act.wait_ge(s["f_projz"], 2 * b + i + 1)
                act.wait_ge(s["f_silu"], b + 1)
                go(th[:, 2 * i:2 * i + 2, :], pair((f_ps, r_ps)[i]), ACT.Tanh, scale=0.5).then_inc(s["f_ztanh"], 1)

            def f_tap(b, c):
                act.wait_ge(s["taps_set"], 1)
                act.wait_ge(s["f_quant"], 2 * b + c // 2 + 1)
                if b:
                    act.wait_ge(s["f_u"], b)
                go(v[:, c, :], q[:, c, TAPS - 1:TAPS - 1 + T], ACT.Identity, bias=conv_b[:, c:c + 1],
                   scale=conv_ws[:, c, TAPS - 1:TAPS]).then_inc(s["f_tap"], 1)

            def f_vtanh(b):
                act.wait_ge(s["f_conv"], 4 * b + 4)
                if b:
                    act.wait_ge(s["f_z"], 2 * b)
                go(th[:, :, :], v[:, :, :], ACT.Tanh, scale=0.5).then_inc(s["f_vtanh"], 1)

            def f_split(b):
                act.wait_ge(s["f_xproj"], b + 1)
                go(b_hi[b % 2][:, :], pair(f_ps, 1), ACT.Copy).then_inc(s["f_bhi"], 1)
                go(dt_in[:, :], pair(f_ps, 0), ACT.Copy, scale=QS).then_inc(s["f_dtin"], 1)

            def f_split2(b):
                act.wait_ge(s["f_brest"], b + 1)
                go(b_mid[64:96, :], b_rest[64:96, :], ACT.Copy)
                go(b_hi[b % 2][32:64, :], b_rest[32:64, :], ACT.Copy).then_inc(s["f_bmid"], 1)

            def f_ccopy(b):
                act.wait_ge(s["f_cproj"], b + 1)
                go(c_t[b % 2][:, :, :], f_ps[:, 0:TT * NS].rearrange("p (a n) -> p a n", a=TT),
                   ACT.Copy).then_inc(s["f_c"], 1)

            def f_abs(b, i):
                act.wait_ge(s["f_dtproj"], 2 * b + i + 1)
                act.wait_ge(s["f_z"], 2 * b + 2)
                for j in range(2):
                    c = 2 * i + j
                    last = go(dt_abs[:, c, :], pair(f_ps, j), ACT.Abs, bias=dt_bias[:, c:c + 1])
                last.then_inc(s["f_abs"], 1)
                act.wait_ge(s["f_abs"], 2 * b + i + 1)
                o = dt_abs[:, 2 * i:2 * i + 2, :]
                go(o, o, ACT.Exp, scale=-1.0).then_inc(s["f_exp"], 1)

            def f_softplus(b):
                act.wait_ge(s["f_exp"], 2 * b + 2)
                go(dt_abs[:, :, :], dt_abs[:, :, :], ACT.Ln, bias=1.0).then_inc(s["f_ln"], 1)

            def copy_b(g):
                act.wait_ge(s["b_spread"], g + 1)
                if g >= BRING:
                    act.wait_ge(s["bu_ready"], 4 * (g - BRING + 1))
                go(b_rep[:, g % BRING, :, :], pair(r_ps), ACT.Copy).then_inc(s["b_copied"], 1)

            def decays(k):
                b, n, c = k // TICKS, (k // 4) % NP, k % 4
                act.wait_ge(s["f_dt"], b + 1)
                act.wait_ge(s["pads_set"], 1)
                if k >= 2:
                    act.wait_ge(s["scanned"], k - 1)
                for j in range(2):
                    last = go(pair(decay[k % 2], j)[:, 1:T], dt[b % 2][:, c, 1:T], ACT.Exp,
                              scale=a_log[:, c, 2 * n + j:2 * n + j + 1])
                last.then_inc(s["decay_ready"], 1)

            def a_qk(b):
                act.wait_ge(s["a_qkmm"], b + 1)
                for i in range(2):
                    go(qk[:, i, :], pair(r_ps, i)[0:H, :], ACT.Identity,
                       bias=b_qk[:, i:i + 1]).then_inc(s["a_qk"], 1)

            def a_scores(b):
                act.wait_ge(s["a_scmm"], b + 1)
                if b:
                    act.wait_ge(s["a_x2"], b)
                go(sc[:, :, :], pair(r_ps), ACT.Copy, scale=H ** -0.5).then_inc(s["a_sc"], 1)

            def a_probs(b):
                act.wait_ge(s["a_max"], b + 1)
                for a in range(TT):
                    last = go(sc[:, a, :], sc[:, a, :], ACT.Exp, bias=a_nm[:, a:a + 1],
                              accum_out=a_sum[:, a:a + 1])
                last.then_inc(s["a_exp"], 1)

            def n_copy(b):
                act.wait_ge(s["n_turned"], b + 1)
                go(xf_t[:, :, :], pair(r_ps), ACT.Copy).then_inc(s["n_xft"], 1)

            def g_exp(b):
                act.wait_ge(s["g_diff"], b + 1)
                go(g_ex[:, :], g_d[:, :], ACT.Exp).then_inc(s["g_exp"], 1)

            def g_hcopy(b):
                act.wait_ge(s["g_hturned"], b + 1)
                go(hot_t[:, :, :], f_ps[:, 0:256].bitcast(BF16).rearrange("p (s t) -> p s t", s=2),
                   ACT.Copy).then_inc(s["g_hcopy"], 1)

            def g_wcopy(b):
                act.wait_ge(s["g_wturned"], b + 1)
                go(w_rep[:, :, :], pair(f_ps), ACT.Copy).then_inc(s["g_wcopy"], 1)

            def ffn_act(b, j):
                (f, _), n = ffn_half(j), 2 * FT * b
                bank = ffn_ps[f % 2]
                act.wait_ge(s["h_mm"], n + j + 1)
                if j == 0:
                    act.wait_ge(s["g_xad"], b + 1)
                if n + j >= 2:
                    act.wait_ge(s["h_gate"], n + j - 1)
                go(ht[:, j % 2, :], pair(bank, 0), ACT.Tanh, scale=0.5).then_inc(s["h_tanh"], 1)
                if n + j >= 2:
                    act.wait_ge(s["h_pair"], n + j - 1)
                go(h3[:, j % 2, :], pair(bank, 1), ACT.Copy).then_inc(s["h_copy"], 1)

            def front(b, age):
                if age == 4:
                    f_xn_copy(b)
                if age in (6, 8):
                    f_xcopy(b, (age - 6) // 2)
                if age in (8, 10):
                    f_tap(b, age - 8)
                    f_tap(b, age - 7)
                if age == 13:
                    f_vtanh(b)
                if age in (15, 17):
                    f_ztanh(b, (age - 15) // 2)
                if age == 18:
                    f_split(b)
                if age == 20:
                    f_split2(b)
                if age == 21:
                    f_ccopy(b)
                if age in (23, 25):
                    f_abs(b, (age - 23) // 2)
                if age == 27:
                    f_softplus(b)

            def rest(b, age):
                if age == 3:
                    a_qk(b)
                if age == 5:
                    a_scores(b)
                if age == 18:
                    a_probs(b)
                if age == 23:
                    n_copy(b)
                if age == 27:
                    g_exp(b)
                if age == 29:
                    g_hcopy(b)
                if age == 30:
                    g_wcopy(b)
                for j in range(2 * FT):
                    if age == ffn_age(j) + 1:
                        ffn_act(b, j)

            for tick in range(FIRST, LAST):
                if tick == FIRST:
                    split_wx()
                if (st := step(tick, -AHEAD)) is not None:
                    decays(st)
                if (st := step(tick, 1 - BAHEAD)) is not None and st % 4 == 0:
                    copy_b(st // 4)
                for b, age in rests(tick):
                    rest(b, age)
                for b, age in fronts(tick):
                    front(b, age)
                if tick == FIRST + 22:
                    hadamard_out()

        @block.gpsimd
        def _(pool):
            tt, ts = nc.gpsimd.tensor_tensor, nc.gpsimd.tensor_scalar

            count = [0]

            def rstd(out, mv):
                count[0] += 1
                ts(out[:, :], mv[:, :, 1], EPS, None, ALU.add).then_inc(s["eps_added"], 1)
                pool.wait_ge(s["eps_added"], count[0])
                return tt(out[:, :], out[:, :], minus_half[:, :], ALU.pow)

            def hadamard4():
                pool.wait_ge(s["ld_out"], LOADED_OUT)
                tmp = yd
                tt(tmp[:, 0::2, :], w_out[:, 0::2, :], w_out[:, 1::2, :], ALU.add).then_inc(s["had_sum"], 1)
                tt(tmp[:, 1::2, :], w_out[:, 0::2, :], w_out[:, 1::2, :], ALU.subtract).then_inc(s["had_sum"], 1)
                pool.wait_ge(s["had_sum"], 2)
                tt(w_bf[:, 0:2, :], tmp[:, 0:2, :], tmp[:, 2:4, :], ALU.add).then_inc(s["had_sum"], 1)
                tt(w_bf[:, 2:4, :], tmp[:, 0:2, :], tmp[:, 2:4, :], ALU.subtract).then_inc(s["had_sum"], 1)

            def scan_input(k):
                b, g, c = k // TICKS, k // 4, k % 4
                pool.wait_ge(s["b_copied"], g + 1)
                pool.wait_ge(s["f_dtu"], b + 1)
                if k >= 3:
                    pool.wait_ge(s["scanned"], k - 2)
                tt(bu[:, k % 3, :, :], b_rep[:, g % BRING, :, :], dtu[b % 2][:, c:c + 1, :].to_broadcast([P, 2, T]),
                   ALU.mult).then_inc(s["bu_ready"], 1)

            def o_gate(b, i):
                pool.wait_ge(s["o_skip"], 2 * b + i + 1)
                tt(yd[:, 2 * i:2 * i + 2, :], yd[:, 2 * i:2 * i + 2, :], zs[b % 2][:, 2 * i:2 * i + 2, :],
                   ALU.mult).then_inc(s["o_gated"], 1)

            def ffn_pair(b, j):
                (f, i), n = ffn_half(j), 2 * FT * b
                pool.wait_ge(s["h_gate"], n + j + 1)
                pool.wait_ge(s["h_copy"], n + j + 1)
                if n + j >= 2:
                    pool.wait_ge(s["h_act"], n + j - 1)
                tt(hg[:, j % 2, :], hg[:, j % 2, :], h3[:, j % 2, :], ALU.mult).then_inc(s["h_pair"], 1)
                pool.wait_ge(s["h_pair"], n + j + 1)
                pool.wait_ge(s["g_wcopy"], b + 1)
                if b:
                    pool.wait_ge(s["p_mm"], b)
                tt(aw[:, f, i, :], hg[:, j % 2, :], w_rep[:, i, :], ALU.mult).then_inc(s["h_act"], 1)
                if i == 1:
                    pool.wait_ge(s["h_act"], n + j + 1)
                    if b:
                        pool.wait_ge(s["e_mm"], b)
                    tt(aws[:, f, :], aw[:, f, 0, :], aw[:, f, 1, :], ALU.add).then_inc(s["h_sum"], 1)

            def p_sum(b):
                pool.wait_ge(s["p_mask"], b + 1)
                tt(p_s, p_m[:, 0, :], p_m[:, 1, :], ALU.add).then_inc(s["p_sum"], 1)

            nc.gpsimd.memset(minus_half[:, :], -0.5).then_inc(s["half_set"], 1)
            pool.wait_ge(s["half_set"], 1)
            def rest(b, age):
                if age in (9, 11):
                    o_gate(b, (age - 9) // 2)
                if age == 15:
                    pool.wait_ge(s["a_var"], b + 1)
                    rstd(a_rs, a_mv).then_inc(s["a_rstd"], 1)
                if age == 20:
                    pool.wait_ge(s["n_var"], b + 1)
                    rstd(n_rs, n_mv).then_inc(s["n_rstd"], 1)
                for j in range(2 * FT):
                    if age == ffn_age(j) + 2:
                        ffn_pair(b, j)
                if age == 50:
                    p_sum(b)

            for tick in range(FIRST, LAST):
                if (st := step(tick, -AHEAD)) is not None:
                    scan_input(st)
                for b, age in rests(tick):
                    rest(b, age)
                for b, age in fronts(tick):
                    if age == 1:
                        pool.wait_ge(s["f_var"], b + 1)
                        rstd(f_rs, f_mv).then_inc(s["f_rstd"], 1)
                if tick == FIRST + 1:
                    hadamard4()

        @block.vector
        def _(dve):
            ve = nc.vector
            tt, ts, stt = ve.tensor_tensor, ve.tensor_scalar, ve.scalar_tensor_tensor
            done = [0]

            def mark(ins):
                done[0] += 1
                ins.then_inc(s["dve_done"], 1)
                return done[0]

            def after(n):
                dve.wait_ge(s["dve_done"], n)

            def setup():
                ve.memset(q[:, :, 0:TAPS - 1], 0.0)
                ve.memset(decay[0][:, :], 0.0)
                ve.memset(decay[1][:, :], 0.0).then_inc(s["pads_set"], 1)

            def setup_weights():
                dve.wait_ge(s["ld_conv"], LOADED_CONV)
                ts(conv_ws[:, :, :], conv_w[:, :, :], QS, None, ALU.mult).then_inc(s["taps_set"], 1)
                dve.wait_ge(s["wx_hi"], 1)
                tt(w_xr[:, :, :], w_x[:, :, :], w_x3[0][:, :, :], ALU.subtract).then_inc(s["wx_rest"], 1)
                dve.wait_ge(s["wx_mid"], 1)
                dve.wait_ge(s["wx_rest"], 1)
                tt(w_x3[2][:, :, :], w_xr[:, :, :], w_x3[1][:, :, :], ALU.subtract).then_inc(s["wx_lo"], 1)

            def setup_masks():
                dve.wait_ge(s["ld_att"], LOADED_ATT)
                for b in range(BATCH):
                    last = tt(masked[:, b, :, :], mask[:, :, :],
                              kmask[:, b:b + 1, :].to_broadcast([P, TT, T]), ALU.max)
                last.then_inc(s["masks_set"], 1)

            def norm_stats(src, st, mv, event):
                for a in range(TT):
                    last = ve.bn_stats(st[:, a, :], src[:, a, :])
                after(mark(last))
                for a in range(TT):
                    last = ve.bn_aggr(mv[:, a, :], st[:, a, :])
                last.then_inc(event, 1)

            def norm(dst, src, mv, rs):
                for a in range(TT):
                    last = ts(dst[:, a, :], src[:, a, :], mv[:, a, 0:1], rs[:, a:a + 1], ALU.subtract, ALU.mult)
                return last

            def f_stats(b):
                dve.wait_ge(ld_xt[b % XBUFS], 16 * (b // XBUFS + 1))
                norm_stats(x_t[b % XBUFS], f_st, f_mv, s["f_var"])

            def f_norm(b):
                dve.wait_ge(s["f_rstd"], b + 1)
                norm(xn, x_t[b % XBUFS], f_mv, f_rs).then_inc(s["f_xn"], 1)

            def f_quant(b, i):
                dve.wait_ge(s["f_xcopy"], 2 * b + i + 1)
                o = xq[:, 2 * i:2 * i + 2, :]
                after(mark(ts(o, o, 127.0, -128.0, ALU.min, ALU.max)))
                ts(q[:, 2 * i:2 * i + 2, TAPS - 1:TAPS - 1 + T], o, MAGIC, MAGIC, ALU.add,
                   ALU.subtract).then_inc(s["f_quant"], 1)

            def f_gate(b, i):
                dve.wait_ge(s["f_ztanh"], 2 * b + i + 1)
                if b >= 2:
                    dve.wait_ge(s["o_gated"], 2 * (b - 1))
                stt(out=zs[b % 2][:, 2 * i:2 * i + 2, :], in0=th[:, 2 * i:2 * i + 2, :], scalar=1.0,
                    in1=pair((f_ps, r_ps)[i]), op0=ALU.add, op1=ALU.mult).then_inc(s["f_z"], 1)

            def f_conv(b, i):
                dve.wait_ge(s["f_tap"], 4 * b + 2 * i + 2)
                n = [0, 0]
                for tap in range(TAPS - 1):
                    for j in range(2):
                        c = 2 * i + j
                        if tap:
                            after(n[j])
                        ins = stt(out=v[:, c, :], in0=q[:, c, tap:tap + T], scalar=conv_ws[:, c, tap:tap + 1],
                                  in1=v[:, c, :], op0=ALU.mult, op1=ALU.add)
                        if tap < TAPS - 2:
                            n[j] = mark(ins)
                        else:
                            ins.then_inc(s["f_conv"], 1)

            def f_silu(b):
                dve.wait_ge(s["f_vtanh"], b + 1)
                stt(out=v[:, :, :], in0=th[:, :, :], scalar=1.0, in1=v[:, :, :],
                    op0=ALU.add, op1=ALU.mult).then_inc(s["f_silu"], 1)

            def f_uquant(b):
                dve.wait_ge(s["f_silu"], b + 1)
                after(mark(ts(v[:, :, :], v[:, :, :], 0.5 / QS, 127.0, ALU.mult, ALU.min)))
                ts(u[b % 2][:, :, :], v[:, :, :], MAGIC, MAGIC, ALU.add, ALU.subtract).then_inc(s["f_u"], 1)

            def f_split(b):
                dve.wait_ge(s["f_bhi"], b + 1)
                dve.wait_ge(s["f_dtin"], b + 1)
                tt(b_rest[:, :], pair(f_ps, 1), b_hi[b % 2][:, :], ALU.subtract).then_inc(s["f_brest"], 1)

            def f_split2(b):
                dve.wait_ge(s["f_bmid"], b + 1)
                tt(b_hi[b % 2][64:96, :], b_rest[64:96, :], b_mid[64:96, :], ALU.subtract).then_inc(s["f_bsplit"], 1)

            def f_pos(b, i):
                dve.wait_ge(s["f_dtproj"], 2 * b + i + 1)
                dve.wait_ge(s["f_abs"], 2 * b + i + 1)
                for j in range(2):
                    c = 2 * i + j
                    last = ts(dt_pos[:, c, :], pair(f_ps, j), dt_bias[:, c:c + 1], 0.0, ALU.add, ALU.max)
                last.then_inc(s["f_pos"], 1)

            def f_dt(b):
                dve.wait_ge(s["f_ln"], b + 1)
                dve.wait_ge(s["f_pos"], 2 * b + 2)
                tt(dt[b % 2][:, :, :], dt_pos[:, :, :], dt_abs[:, :, :], ALU.add).then_inc(s["f_dt"], 1)

            def f_dtu(b):
                dve.wait_ge(s["f_dt"], b + 1)
                stt(out=dtu[b % 2][:, :, :], in0=dt[b % 2][:, :, :], scalar=QS * QS, in1=u[b % 2][:, :, :],
                    op0=ALU.mult, op1=ALU.mult).then_inc(s["f_dtu"], 1)

            def scan(k):
                g, c = k // 4, k % 4
                dve.wait_ge(s["decay_ready"], k + 1)
                dve.wait_ge(s["bu_ready"], k + 1)
                if g >= HRING:
                    dve.wait_ge(s["turned"], 4 * (g - HRING + 1))
                ve.tensor_tensor_scan(h[:, g % HRING, c, :, :].rearrange("p n t -> p (n t)"), decay[k % 2][:, :],
                                      bu[:, k % 3, :, :].rearrange("p n t -> p (n t)"), 0.0,
                                      ALU.mult, ALU.add).then_inc(s["scanned"], 1)

            def weigh(k):
                b, n, a = k // TICKS, 2 * ((k // 4) % NP) + (k // 2) % 2, k % 2
                dst, src, c = acc[b % 2][:, a, :], h_t[k % 2][:, :], c_t[b % 2][:, a, n:n + 1]
                dve.wait_ge(s["turned"], k + 1)
                dve.wait_ge(s["f_c"], b + 1)
                if n == 0:
                    if b >= 2:
                        dve.wait_ge(s["o_turned"], 2 * (b - 1))
                    ts(dst, src, c, None, ALU.mult).then_inc(s["weighted"], 1)
                else:
                    dve.wait_ge(s["weighted"], k - 1)
                    stt(out=dst, in0=src, scalar=c, in1=dst, op0=ALU.mult, op1=ALU.add).then_inc(s["weighted"], 1)

            def o_skip(b, i):
                dve.wait_ge(s["o_turned"], 2 * b + i + 1)
                for j in range(2):
                    c = 2 * i + j
                    last = stt(out=yd[:, c, :], in0=u[b % 2][:, c, :], scalar=d_skip[:, c:c + 1],
                               in1=pair(r_ps, j), op0=ALU.mult, op1=ALU.add)
                last.then_inc(s["o_skip"], 1)

            def o_x1(b):
                dve.wait_ge(s["o_mm"], 2 * b + 2)
                tt(x1[:, :, :], pair(r_ps), x_t[b % XBUFS][:, :, :], ALU.add).then_inc(s["o_x1"], 1)

            def a_stats(b):
                dve.wait_ge(s["o_x1"], b + 1)
                norm_stats(x1, a_st, a_mv, s["a_var"])

            def a_gate(b):
                dve.wait_ge(s["a_rstd"], b + 1)
                dve.wait_ge(s["a_sc"], b + 1)
                n = mark(norm(qc, x1, a_mv, a_rs))
                after(n)
                tt(sc[:, :, :], sc[:, :, :], qc[:, :, :], ALU.mult).then_inc(s["a_gated"], 1)

            def a_mask(b):
                dve.wait_ge(s["a_gated"], b + 1)
                dve.wait_ge(s["masks_set"], 1)
                after(mark(stt(out=sc[:, :, :], in0=masked[:, b, :, :], scalar=MASKED, in1=sc[:, :, :],
                               op0=ALU.mult, op1=ALU.add)))
                after(mark(ve.tensor_reduce(a_mx[:, :], sc[:, :, :], AX.X, ALU.max)))
                ts(a_nm[:, :], a_mx[:, :], -1.0, None, ALU.mult).then_inc(s["a_max"], 1)

            def a_x2(b):
                dve.wait_ge(s["a_exp"], b + 1)
                after(mark(ve.reciprocal(a_rec[:, :], a_sum[:, :])))
                if b >= 2:
                    dve.wait_ge(s["stored"], 16 * (b - 1))
                for a in range(TT):
                    last = stt(out=x2[b % 2][:, a, :], in0=sc[:, a, :], scalar=a_rec[:, a:a + 1], in1=x1[:, a, :],
                               op0=ALU.mult, op1=ALU.add)
                last.then_inc(s["a_x2"], 1)
                dve.wait_ge(s["a_x2"], b + 1)
                norm_stats(x2[b % 2], n_st, n_mv, s["n_var"])

            def n_norm(b):
                dve.wait_ge(s["n_rstd"], b + 1)
                norm(xf, x2[b % 2], n_mv, n_rs).then_inc(s["n_xf"], 1)

            def g_top(b):
                dve.wait_ge(s["g_mm"], b + 1)
                ve.tensor_copy(lg[:, :, :], r_ps[:, 0:TT * E].rearrange("p (a e) -> p a e", a=TT)).then_inc(s["g_lg"], 1)
                dve.wait_ge(s["g_lg"], b + 1)
                for a in range(TT):
                    last = ve.max(out=top[:, a, :], in_=lg[:, a, :])
                after(mark(last))
                tt(g_d[:, :], top[:, :, 1], top[:, :, 0], ALU.subtract).then_inc(s["g_diff"], 1)
                for a in range(TT):
                    last = ve.max_index(out=topi[:, a, :], in_max=top[:, a, :], in_values=lg[:, a, :])
                after(mark(last))
                after(mark(ve.tensor_copy(topf[:, :, :], topi[:, :, :])))
                for i in range(2):
                    for a in range(TT):
                        last = ts(hot[:, i, a, :], rank_expert[:, :], topf[:, a, i:i + 1], None, ALU.is_equal)
                last.then_inc(s["g_hot"], 1)

            def g_weights(b):
                dve.wait_ge(s["g_exp"], b + 1)
                after(mark(ts(g_one[:, :], g_ex[:, :], 1.0, None, ALU.add)))
                after(mark(ve.reciprocal(g_rec[:, :], g_one[:, :])))
                ts(g_w[:, 0, :], g_rec[:, :], 0.5, None, ALU.mult)
                stt(out=g_w[:, 1, :], in0=g_rec[:, :], scalar=0.5, in1=g_ex[:, :], op0=ALU.mult,
                    op1=ALU.mult).then_inc(s["g_wts"], 1)

            def g_select(b):
                dve.wait_ge(s["g_hcopy"], b + 1)
                dve.wait_ge(s["g_xa"], b + 1)
                n = mark(tt(hot_d, hot_t[:, 1, :], hot_t[:, 0, :], ALU.subtract))
                for o in range(2):
                    last = stt(out=xa1[:, o, :], in0=pair(r_ps, o), scalar=2.0, in1=hot_t[:, 0, :],
                               op0=ALU.mult, op1=ALU.mult)
                last.then_inc(s["g_xa1"], 1)
                after(n)
                for o in range(2):
                    last = stt(out=xad[:, o, :], in0=pair(r_ps, o), scalar=2.0, in1=hot_d,
                               op0=ALU.mult, op1=ALU.mult)
                last.then_inc(s["g_xad"], 1)

            def ffn_gate(b, j):
                (f, _), n = ffn_half(j), 2 * FT * b
                dve.wait_ge(s["h_tanh"], n + j + 1)
                dve.wait_ge(s["h_copy"], n + j + 1)
                if n + j >= 2:
                    dve.wait_ge(s["h_act"], n + j - 1)
                stt(out=hg[:, j % 2, :], in0=ht[:, j % 2, :], scalar=1.0, in1=pair(ffn_ps[f % 2], 0),
                    op0=ALU.add, op1=ALU.mult).then_inc(s["h_gate"], 1)

            def p_mask(b):
                dve.wait_ge(s["p_mm"], b + 1)
                stt(out=p_m[:, :, :], in0=pair(ffn_ps[0]), scalar=2.0, in1=hot_t[:, :, :], op0=ALU.mult,
                    op1=ALU.mult).then_inc(s["p_mask"], 1)

            def e_out(b):
                dve.wait_ge(s["e_mm"], b + 1)
                o = x2[b % 2]
                tt(o[:, :, :], pair(ffn_ps[1]), o[:, :, :], ALU.add).then_inc(s["e_done"], 1)

            setup()

            def front(b, age):
                if age == 0:
                    f_stats(b)
                if age == 2:
                    f_norm(b)
                if age in (7, 9):
                    f_quant(b, (age - 7) // 2)
                if age in (9, 11):
                    f_conv(b, (age - 9) // 2)
                if age == 14:
                    f_silu(b)
                if age == 15:
                    f_uquant(b)
                if age in (16, 18):
                    f_gate(b, (age - 16) // 2)
                if age == 19:
                    f_split(b)
                if age == 21:
                    f_split2(b)
                if age in (24, 26):
                    f_pos(b, (age - 24) // 2)
                if age == 28:
                    f_dt(b)
                if age == 29:
                    f_dtu(b)

            def rest(b, age):
                if age in (8, 10):
                    o_skip(b, (age - 8) // 2)
                if age == 14:
                    o_x1(b)
                    a_stats(b)
                if age == 16:
                    a_gate(b)
                if age == 17:
                    a_mask(b)
                if age == 19:
                    a_x2(b)
                if age == 21:
                    n_norm(b)
                if age == 25:
                    g_top(b)
                if age == 28:
                    g_weights(b)
                if age == 30:
                    g_select(b)
                for j in range(2 * FT):
                    if age == ffn_age(j) + 1:
                        ffn_gate(b, j)
                if age == 50:
                    p_mask(b)
                if age == 52:
                    e_out(b)

            for tick in range(FIRST, LAST):
                if (st := step(tick, 0)) is not None:
                    scan(st)
                if (st := step(tick, CLAG)) is not None:
                    weigh(st)
                for b, age in rests(tick):
                    rest(b, age)
                for b, age in fronts(tick):
                    front(b, age)
                if tick == FIRST + 2:
                    setup_weights()
                if tick == FIRST + 22:
                    setup_masks()


def kernel(**inputs):
    import numpy as np
    import ml_dtypes
    import concourse.bacc as bacc
    from concourse.bass_utils import run_bass_kernel_spmd

    a = {k: np.asarray(v) for k, v in inputs.items()}

    def rows(w):
        return w.reshape(-1, P, w.shape[-1]).transpose(1, 0, 2)

    def col(vec):
        return vec.reshape(-1, P).T

    def pad(w, axis):
        widths = [(0, 0)] * w.ndim
        widths[axis] = (0, FT * P - FF)
        return np.pad(w, widths)

    w_x = a["L0_attn_W_x"].T
    wide = np.zeros((DI, 2 * P + NS), w_x.dtype)
    wide[:, 0:P] = w_x[:, 0:P]
    for i in range(3):
        wide[:, P + 32 * i:P + 32 * i + NS] = w_x[:, P:P + NS]
    wide[:, 2 * P:] = w_x[:, P + NS:]

    ident = np.eye(P, dtype=np.float32)
    had = np.ones((1, 1), np.float32)
    while had.shape[0] < P:
        had = np.block([[had, had], [had, -had]])
    sel = np.zeros((P, NS), ml_dtypes.bfloat16)
    for n in range(NS):
        for i in range(3):
            sel[32 * i + n, n] = 1
    rank_expert = np.repeat(np.arange(E, dtype=np.float32), R)[None, :].repeat(P, 0)

    arrays = {
        "x": a["x"],
        "ident": ident, "identb": ident.astype(ml_dtypes.bfloat16), "had": had, "sel": sel,
        "rank_expert": rank_expert,
        "w_in": rows(a["L0_attn_W_in"].T),
        "conv_w": a["L0_attn_conv_w"].reshape(CT, P, TAPS).transpose(1, 0, 2),
        "conv_b": col(a["L0_attn_conv_b"]),
        "w_x": rows(wide),
        "w_dt": a["L0_attn_W_dt"].T,
        "dt_bias": col(a["L0_attn_dt_bias"]),
        "a_log": a["L0_attn_A"].reshape(CT, P, NS).transpose(1, 0, 2),
        "d_skip": col(a["L0_attn_D"]),
        "w_out": rows(a["L0_attn_W_out"].T),
        "ctx_t": a["ctx_512"].transpose(2, 0, 1),
        "w_q": a["L0_xattn_Wq"].T, "w_k": a["L0_xattn_Wk"].T,
        "b_qk": np.stack([a["L0_xattn_bq"], a["L0_xattn_bk"]], 1),
        "mask": a["mask_SxS2_bk1"].reshape(TT, P, T).transpose(1, 0, 2),
        "kmask": np.broadcast_to(a["mask_BxS2_bf0"][None], (P, BATCH, T)),
        "gate": rows(a["L0_ffn_gate_w"].T),
        "w1": rows(pad(a["L0_ffn_w1"], 0).T), "w3": rows(pad(a["L0_ffn_w3"], 0).T),
        "w2": rows(pad(a["L0_ffn_w2"], 1).T),
        "la1": rows(a["L0_ffn_a1"].reshape(E * R, D).T), "la3": rows(a["L0_ffn_a3"].reshape(E * R, D).T),
        "lb1": pad(a["L0_ffn_b1"], 1).transpose(0, 2, 1).reshape(E * R, FT * P),
        "lb3": pad(a["L0_ffn_b3"], 1).transpose(0, 2, 1).reshape(E * R, FT * P),
        "la2": rows(pad(a["L0_ffn_a2"], 2).reshape(E * R, FT * P).T),
        "lb2": a["L0_ffn_b2"].transpose(0, 2, 1).reshape(E * R, D),
    }
    arrays = {f"in_{k}": np.ascontiguousarray(v) for k, v in arrays.items()}
    nc = bacc.Bacc("TRN2", target_bir_lowering=False, num_devices=1)
    t = {k[3:]: nc.dram_tensor(k, v.shape, mybir.dt.from_np(v.dtype), kind="ExternalInput").ap()
         for k, v in arrays.items()}
    t["out"] = nc.dram_tensor("out_0", (BATCH, T, D), F32, kind="ExternalOutput").ap()
    build(nc, t)
    r = run_bass_kernel_spmd(nc, [arrays], core_ids=[0])
    return r.results[0]["out_0"]
```

```python
from contextlib import ExitStack

import concourse.bass as bass
from concourse import mybir

F32 = mybir.dt.float32
BF16 = mybir.dt.bfloat16
U8 = mybir.dt.uint8
U32 = mybir.dt.uint32
ALU = mybir.AluOpType
ACT = mybir.ActivationFunctionType
AX = mybir.AxisListType

P = 128
BATCH, T, D = 4, 256, 256
TT = T // P
DK = D // P
DI = 512
CT = DI // P
NS = 16
NP = NS // 2
TAPS = 4
H = 64
E, R = 8, 16
FF = 704
FT = -(-FF // P)
EPS = 1e-5
QS = 0.05
MAGIC = 1.5 * 2.0 ** 23
MASKED = -1e30

STEPS = CT * NP
HRING = 10
BRING = 3

SMALL = ((1, P), (CT, TAPS), (1, CT), (1, CT), (CT, NS), (1, CT))
BITS = ((1, P), (1, NS))
ATT = ((BATCH, T), (1, H), (1, H), (1, 2))
FFN = ((DK, E), (DK, P), (DK, P), (1, P), (DK, FT * P), (DK, FT * P), (1, FT * P), (1, FT * P), (FT, D),
       (FT, P), (1, D))

SLOT = 2 * STEPS
DECAY, INPUT, SPREAD, COPY_B, TURN, WEIGH = -2, -3, -13, -12, 11, 13
LEAD = SLOT + 8
TAIL = 194
FIRST, LAST = -LEAD, BATCH * SLOT + TAIL
AT = {
    "act.split_wx": (6,), "dve.setup_weights": (0,), "dve.setup_masks": (63,), "pool.hadamard4": (25,),
    "pe.hadamard_out": (58,), "act.hadamard_out": (62,), "dve.setup_conv": (0,), "dve.setup_wx": (10,),
    "pe.f_turn": (2,), "pe.f_proj_x": (6, 7), "pe.f_conv": (12, 20), "pe.f_proj_z": (37, 45),
    "pe.f_xproj": (39, 42), "pe.f_cproj": (45,), "pe.f_dtproj": (47, 51),
    "pe.a_qk": (6,), "pe.a_scores": (14,), "pe.o_turn": (18, 21), "pe.o_proj": (23, 25), "pe.n_turn": (46,),
    "pe.g_logits": (53,), "pe.g_lora": (55,), "pe.g_turn_hot": (55,), "pe.g_turn_e": (56,),
    "pe.ffn_base": (58, 60, 71, 80, 86, 90), "pe.ffn_lora": (58, 63, 67, 70, 75, 80, 81, 85, 86, 93, 97, 99),
    "pe.ffn_ranks": (102, 104, 105), "pe.ffn_down": (105, 110, 112, 116), "pe.ffn_down_lora": (121,),
    "act.f_xn_copy": (3,), "act.f_xcopy": (8, 11), "act.f_q": (10, 17), "act.f_tap": (11, 12, 25, 26),
    "act.f_vtanh": (23, 34), "act.f_u": (36, 39), "act.f_ztanh": (40, 46), "act.f_split": (44,),
    "act.f_ccopy": (46,), "act.f_abs": (51, 60), "act.f_split2": (53,), "act.f_exp": (55, 63),
    "act.f_softplus": (64,),
    "act.a_qk": (6,), "act.a_scores": (17,), "act.a_probs": (41,), "act.n_copy": (51,), "act.g_exp": (56,),
    "act.g_hcopy": (56,), "act.g_ecopy": (57,), "act.ffn_act": (60, 67, 68, 73, 76, 83, 84, 85, 86, 97, 99, 104),
    "pool.f_rstd": (0,),
    "pool.o_gate": (21, 22), "pool.a_rstd": (33,), "pool.n_rstd": (41,), "pool.hot_e": (61,),
    "pool.ffn_pair": (63, 71, 75, 81, 81, 83, 87, 89, 98, 100, 104, 105), "pool.p_sum": (122,),
    "dve.f_stats": (0,), "dve.f_norm": (1,), "dve.f_clip": (9, 13), "dve.f_conv": (14, 28), "dve.f_silu": (30, 35),
    "dve.f_uclip": (33, 36), "dve.f_gate": (42, 48), "dve.f_split": (45,), "dve.f_split2": (58,),
    "dve.f_dt": (66, 67), "dve.f_dtu": (66, 71),
    "dve.o_skip": (19, 21), "dve.o_x1": (28,), "dve.a_stats": (29,), "dve.a_gate": (36,), "dve.a_mask": (38,),
    "dve.a_x2": (40,), "dve.n_stats": (41,), "dve.n_norm": (44,), "dve.g_hot": (54,), "dve.g_top": (54,),
    "dve.g_select": (57,), "dve.ffn_gate": (63, 67, 71, 78, 82, 83, 85, 89, 91, 98, 100, 104),
    "dve.g_weights": (89,), "dve.p_mask": (108,), "dve.e_out": (123,),
}
AT_FIRST = {
    "pe.f_proj_x": (0, 10), "pe.f_turn": (0,), "pe.f_conv": (15, 23), "pe.f_proj_z": (31, 45),
    "pe.f_xproj": (33, 40), "pe.f_cproj": (49,), "pe.f_dtproj": (51, 53),
    "act.f_xn_copy": (0,), "act.f_xcopy": (3, 10), "act.f_q": (8, 14), "act.f_tap": (10, 13, 27, 29),
    "act.f_vtanh": (30, 36), "act.f_ztanh": (40, 50), "act.f_u": (43, 44), "act.f_split": (45,),
    "act.f_ccopy": (48,), "act.f_abs": (51, 52), "act.f_split2": (52,), "act.f_exp": (54, 65),
    "act.f_softplus": (66,),
    "dve.f_norm": (0,), "dve.f_clip": (10, 11), "dve.f_conv": (12, 18), "dve.f_silu": (36, 36),
    "dve.f_uclip": (36, 41), "dve.f_gate": (47, 52), "dve.f_split": (51,), "dve.f_split2": (56,),
    "dve.f_dt": (70, 71), "dve.f_dtu": (70, 71),
}
AT_LATE = {
    "pe.a_qk": (4,), "pe.a_scores": (11,), "pe.o_proj": (22, 23), "pe.g_logits": (50,), "pe.g_lora": (56,),
    "pe.g_turn_hot": (56,), "pe.g_turn_e": (57,), "pe.ffn_base": (58, 61, 72, 79, 86, 90),
    "pe.ffn_lora": (58, 64, 69, 69, 74, 79, 81, 85, 86, 91, 97, 100), "pe.ffn_ranks": (101, 104, 104),
    "pe.ffn_down": (105, 109, 110, 112), "pe.ffn_down_lora": (120,),
    "act.a_scores": (16,), "act.a_probs": (40,), "act.n_copy": (47,), "act.g_exp": (54,), "act.g_ecopy": (56,),
    "act.ffn_act": (61, 68, 69, 69, 74, 78, 79, 80, 81, 96, 99, 104),
    "pool.o_gate": (19, 21), "pool.a_rstd": (32,),
    "pool.ffn_pair": (64, 71, 74, 81, 81, 86, 90, 90, 95, 99, 101, 101), "pool.p_sum": (116,),
    "dve.o_skip": (20, 22), "dve.o_x1": (26,), "dve.g_top": (51,), "dve.g_select": (58,),
    "dve.ffn_gate": (64, 69, 71, 77, 82, 83, 85, 89, 91, 97, 98, 104), "dve.g_weights": (91,), "dve.p_mask": (105,),
    "dve.e_out": (120,),
}
AT_LAST = {
    "pe.a_qk": (1,), "pe.o_turn": (19, 21), "pe.o_proj": (22, 23), "pe.g_lora": (56,),
    "pe.ffn_base": (58, 60, 69, 85, 98, 99), "pe.g_turn_hot": (58,),
    "pe.ffn_lora": (60, 60, 67, 67, 69, 86, 91, 97, 98, 101, 126, 126), "pe.g_turn_e": (65,),
    "pe.ffn_ranks": (133, 147, 169), "pe.ffn_down": (179, 180, 180, 181), "pe.ffn_down_lora": (193,),
    "act.a_qk": (0,), "act.a_scores": (11,), "act.a_probs": (51,), "act.n_copy": (56,), "act.g_exp": (57,),
    "act.g_hcopy": (57,), "act.ffn_act": (61, 64, 71, 83, 90, 123, 123, 124, 124, 124, 160, 174),
    "act.g_ecopy": (68,),
    "pool.o_gate": (17, 19), "pool.a_rstd": (29,),
    "pool.ffn_pair": (56, 61, 69, 81, 81, 88, 94, 95, 124, 125, 162, 175), "pool.hot_e": (83,),
    "pool.p_sum": (185,),
    "dve.o_skip": (20, 24), "dve.a_gate": (34,), "dve.a_mask": (37,), "dve.n_stats": (40,), "dve.g_hot": (55,),
    "dve.g_top": (55,), "dve.g_select": (60,),
    "dve.ffn_gate": (62, 67, 69, 85, 91, 91, 96, 109, 130, 181, 181, 182), "dve.g_weights": (96,),
    "dve.p_mask": (189,), "dve.e_out": (192,),
}


def build(nc, t):
    with ExitStack() as ctx:
        def sb(name, shape, dt=F32):
            return ctx.enter_context(nc.sbuf_tensor(name, shape, dt))

        def psum(name):
            return ctx.enter_context(nc.psum_tensor(name, [P, 512], F32))

        def sems(names):
            return {n: ctx.enter_context(nc.semaphore(n)) for n in names.split()}

        def packed(name, partitions, dtype, parts):
            tile = sb(name, [partitions, sum(n * m for n, m in parts)], dtype)
            views, at = [], 0
            for n, m in parts:
                view = tile[:, at:at + n * m]
                views.append(view if n == 1 else view.rearrange("p (n m) -> p n m", n=n))
                at += n * m
            return tile, views

        small, (ident, conv_w, conv_b, dt_bias, a_log, d_skip) = packed("small", P, F32, SMALL)
        bits, (identb, sel) = packed("bits", P, BF16, BITS)
        att, (ctx_t, w_q, w_k, b_qk) = packed("att", H, F32, ATT)
        ffn, (gate, la1, la3, rank_expert, w1, w3, lb1, lb3, w2, la2, lb2) = packed("ffn", P, F32, FFN)
        had = sb("had", [P, P])
        conv_bs = sb("conv_bs", [P, CT])
        NT = TAPS - 1
        conv_part = sb("conv_part", [P, CT, 3, NT], BF16)
        conv_rest = sb("conv_rest", [P, CT, NT])
        conv_d = sb("conv_d", [P, CT, 3, NT, P], BF16)
        w_in = sb("w_in", [P, DK, 2 * DI])
        conv_ws = sb("conv_ws", [P, CT, TAPS])
        WX = 2 * P + NS
        w_x3 = [sb(f"w_x3_{i}", [P, CT, WX], BF16) for i in range(3)]
        w_dt = sb("w_dt", [P, DI])
        w_oh = sb("w_oh", [P, CT, D])
        masked = sb("masked", [P, BATCH, TT, T], U8)

        minus_half = sb("minus_half", [P, TT])
        magic = sb("magic", [P, 2])

        x_t = sb("x_t", [P, TT, D])
        f_st = sb("f_st", [P, TT, 6])
        f_mv = sb("f_mv", [P, TT, 2])
        f_rs = sb("f_rs", [P, TT])
        xn_t = sb("xn_t", [P, DK, T])
        q = sb("q", [P, CT, TAPS - 1 + T], BF16)
        v = sb("v", [P, CT, T])
        zs = [sb(f"zs{i}", [P, CT, T]) for i in range(2)]
        u = [sb(f"u{i}", [P, CT, T], BF16) for i in range(2)]
        dt_in = sb("dt_in", [P, T])
        b_hi = [sb(f"b_hi{i}", [P, T], BF16) for i in range(2)]
        b_rest = sb("b_rest", [P, T])
        b_mid = sb("b_mid", [P, T], BF16)
        c_t = [sb(f"c_t{i}", [P, TT, NS]) for i in range(2)]
        dt_abs = sb("dt_abs", [P, CT, T])
        xq = th = dt_abs
        dt_pos = v
        dt = [sb(f"dt{i}", [P, CT, T]) for i in range(2)]
        dtu = [sb(f"dtu{i}", [P, CT, T]) for i in range(2)]

        b_rep = sb("b_rep", [P, BRING, 2, T])
        bu = sb("bu", [P, 3, 2, T])
        h = sb("h", [P, HRING, 2, T])
        acc = [sb(f"acc{i}", [P, TT, DI]) for i in range(2)]

        yd = sb("yd", [P, CT, T])
        x_res = sb("x_res", [P, TT, D])
        x1 = sb("x1", [P, TT, D])
        qk = sb("qk", [H, 2, T])
        sc = sb("sc", [P, TT, T])
        a_st = sb("a_st", [P, TT, 6])
        a_mv = sb("a_mv", [P, TT, 2])
        a_rs = sb("a_rs", [P, TT])
        a_mx = sb("a_mx", [P, TT])
        a_nm = sb("a_nm", [P, TT])
        a_sum = sb("a_sum", [P, TT])
        a_rec = sb("a_rec", [P, TT])
        x2 = [sb(f"x2_{i}", [P, TT, D]) for i in range(2)]
        n_st = sb("n_st", [P, TT, 6])
        n_mv = sb("n_mv", [P, TT, 2])
        n_rs = sb("n_rs", [P, TT])
        xf = sb("xf", [P, TT, D])
        qc = xf
        xf_t = sb("xf_t", [P, DK, T])
        lg = sb("lg", [P, TT, E])
        top = sb("top", [P, TT, 8])
        topi = sb("topi", [P, TT, 8], U32)
        topf = sb("topf", [P, TT, 8])
        g_d = sb("g_d", [P, TT])
        g_ex = sb("g_ex", [P, TT])
        g_one = sb("g_one", [P, TT])
        g_w = sb("g_w", [P, 2, TT])
        hot = sb("hot", [P, 2, TT, P], BF16)
        hot_t = sb("hot_t", [P, 2, T])
        e_rep = sb("e_rep", [P, T])
        xa1 = sb("xa1", [P, 2, T])
        xad = sb("xad", [P, 2, T])
        ht = sb("ht", [P, 2, T])
        h3 = sb("h3", [P, 2, T])
        hot_d = h3[:, 0, :]
        hg = sb("hg", [P, 2, T])
        aw = sb("aw", [P, FT, 2, T])
        aws = sb("aws", [P, FT, T])
        p_m = xa1
        p_s = ht[:, 0, :]
        w_x, w_xr = (h[:, :, :, :].rearrange("p k n t -> p (k n t)")[:, i * CT * WX:(i + 1) * CT * WX].rearrange(
            "p (c n) -> p c n", c=CT) for i in range(2))
        masks = aws[:, :, :].rearrange("p f t -> p (f t)")[:, 0:(TT + BATCH) * T // 4].bitcast(U8).rearrange(
            "p (a t) -> p a t", a=TT + BATCH)
        mask, kmask = masks[:, 0:TT, :], masks[:, TT:, :]
        w_out, w_bf = (aw[:, 2 * i:2 * i + 2, :, :].rearrange("p f i t -> p (f i) t") for i in range(2))

        decay = [psum(f"decay{i}") for i in range(2)]
        h_t = [psum(f"h_t{i}") for i in range(2)]
        work = [psum(f"work{i}") for i in range(4)]
        f_ps, r_ps, ffn_ps = work[0], work[1], work[2:4]

        s = sems(
            "ld_xt ld_res ld_small ld_in ld_x ld_dt ld_bits ld_out ld_had ld_att ld_masks ld_ffn stored "
            "half_set eps_added pads_set taps_set conv_set wx_hi wx_rest wx_mid wx_lo had_sum had_mm had_done "
            "masks_set "
            "f_var f_rstd f_xn f_turned f_xn_t f_projx f_projz f_xcopy f_clip f_quant f_tap f_convmm f_conv "
            "f_ztanh f_z "
            "f_vtanh f_silu f_uclip f_u f_xproj f_cproj f_dtin f_bhi f_brest f_bmid f_bsplit f_c f_dtproj "
            "f_abs f_pos f_exp f_ln f_dt f_dtu "
            "b_spread b_copied bu_ready decay_ready scanned turned weighted "
            "o_turned o_skip o_gated o_mm o_x1 a_qkmm a_qk a_scmm a_sc a_var a_rstd a_gated a_max a_exp a_x2 "
            "n_var n_rstd n_xf n_turned n_xft g_mm g_lg g_xa g_diff g_exp g_hot g_hturned g_hcopy "
            "g_eturned g_ecopy g_xa1 g_xad g_hot_e h_mm h_tanh h_copy h_gate h_act h_scaled h_sum p_mm p_mask "
            "p_sum e_mm e_done "
            "dve_done")

        def pair(bank, i=None):
            v2 = bank[:, :].rearrange("p (a t) -> p a t", a=2)
            return v2 if i is None else v2[:, i, :]

        def step(beat, offset):
            k, odd = divmod(beat - offset, 2)
            return k if not odd and 0 <= k < BATCH * STEPS else None

        def ffn_half(j):
            return 2 * (j // 4) + j % 2, (j // 2) % 2

        def fronts(beat):
            ages = [(b, beat - SLOT * b + LEAD) for b in range(BATCH)]
            return [(b, age) for b, age in ages if 0 <= age < LEAD]

        def rests(beat):
            ages = [(b, beat - SLOT * (b + 1)) for b in range(BATCH)]
            return [(b, age) for b, age in ages if 0 <= age < TAIL]

        def due(piece, age, b=None):
            own = {0: AT_FIRST, BATCH - 2: AT_LATE, BATCH - 1: AT_LAST}.get(b, {})
            return [i for i, at in enumerate(own.get(piece, AT[piece])) if at == age]

        block = ctx.enter_context(nc.Block())

        @block.sync
        def _(sp):
            def load(tile, name, event):
                sp.dma_start(tile, t[name]).then_inc(s[event], 16)

            def x_load(b):
                if b:
                    sp.wait_ge(s["f_turned"], b)
                sp.dma_start(x_t[:, :, :], t["x"][b].rearrange("(a p) d -> p a d", p=P)).then_inc(s["ld_xt"], 16)

            def res_load(b):
                if b:
                    sp.wait_ge(s["o_x1"], b)
                sp.dma_start(x_res[:, :, :], t["x"][b].rearrange("(a p) d -> p a d", p=P)).then_inc(s["ld_res"], 16)

            def store(b):
                sp.wait_ge(s["e_done"], b + 1)
                sp.dma_start(t["out"][b].rearrange("(a p) d -> p a d", p=P),
                             x2[b % 2][:, :, :]).then_inc(s["stored"], 16)

            x_load(0)
            load(small[:, :], "small", "ld_small")
            load(bits[:, :], "bits", "ld_bits")
            load(w_in[:, :, :], "w_in", "ld_in")
            load(w_x[:, :, :], "w_x", "ld_x")
            load(w_dt[:, :], "w_dt", "ld_dt")
            load(w_out[:, :, :], "w_out", "ld_out")
            load(had[:, :], "had", "ld_had")
            x_load(1)
            res_load(0)
            load(att[:, :], "att", "ld_att")
            load(masks[:, :, :], "masks", "ld_masks")
            load(ffn[:, :], "ffn", "ld_ffn")
            x_load(2)
            x_load(3)
            res_load(1)
            res_load(2)
            store(0)
            res_load(3)
            for b in range(1, BATCH):
                store(b)
            sp.wait_ge(s["stored"], 16 * BATCH)

        @block.tensor
        def _(pe):
            mm, turn = nc.tensor.matmul, nc.tensor.transpose

            readers = {}

            def take(bank, *events):
                for event, count in readers.get(id(bank), ()):
                    pe.wait_ge(s[event], count)
                readers[id(bank)] = events

            def hadamard_out():
                pe.wait_ge(s["ld_had"], 16)
                pe.wait_ge(s["had_sum"], 4)
                for i in range(2):
                    take(ffn_ps[i], ("had_done", i + 1))
                    for j in range(2):
                        last = mm(pair(ffn_ps[i], j), had[:, :], w_bf[:, 2 * i + j, :], start=True, stop=True)
                    last.then_inc(s["had_mm"], 1)

            def f_turn(b):
                pe.wait_ge(s["ld_small"], 16)
                pe.wait_ge(s["f_xn"], b + 1)
                take(f_ps, ("f_xn_t", b + 1))
                for k in range(DK):
                    for a in range(TT):
                        last = turn(pair(f_ps, k)[:, a * P:a * P + P], x_t[:, a, k * P:k * P + P], ident[:, :])
                last.then_inc(s["f_turned"], 1)

            def project(bank, b, i):
                pe.wait_ge(s["ld_in"], 16)
                pe.wait_ge(s["f_xn_t"], b + 1)
                for j in range(2):
                    c = 2 * i + j
                    for k in range(DK):
                        last = mm(pair(bank, j), w_in[:, k, c * P:c * P + P], xn_t[:, k, :],
                                  start=(k == 0), stop=(k == DK - 1))
                return last

            def f_proj_x(b, i):
                take(f_ps, ("f_xcopy", 2 * b + i + 1))
                project(f_ps, b, i).then_inc(s["f_projx"], 1)

            def f_conv(b, i):
                pe.wait_ge(s["conv_set"], 2 * i + 2)
                pe.wait_ge(s["f_quant"], 2 * b + i + 1)
                take(f_ps, ("f_conv", 2 * b + i + 1))
                for j in range(2):
                    c = 2 * i + j
                    for tap in range(NT):
                        for part in range(3):
                            last = mm(pair(f_ps, j), conv_d[:, c, part, tap, :], q[:, c, tap:tap + T],
                                      start=(tap == 0 and part == 0), stop=(tap == NT - 1 and part == 2))
                last.then_inc(s["f_convmm"], 1)

            def f_proj_z(b, i):
                bank = r_ps
                take(bank, ("f_ztanh", 2 * b + i + 1), ("f_z", 2 * b + i + 1))
                project(bank, b, 2 + i).then_inc(s["f_projz"], 1)

            def f_xproj(b, j):
                pe.wait_ge(s["wx_lo"], 1)
                pe.wait_ge(s["f_u"], 2 * b + 2)
                if j == 0:
                    take(f_ps, ("f_dtin", b + 1), ("f_bhi", b + 1), ("f_brest", b + 1))
                n = 0
                for k in range(CT):
                    for part in w_x3:
                        last = mm(pair(f_ps, j), part[:, k, j * P:j * P + P], u[b % 2][:, k, :],
                                  start=(n == 0), stop=(n == 3 * CT - 1))
                        n += 1
                last.then_inc(s["f_xproj"], 1)

            def f_cproj(b):
                take(f_ps, ("f_c", b + 1))
                for a in range(TT):
                    n = 0
                    for k in range(CT):
                        for part in w_x3:
                            last = mm(f_ps[:, a * NS:a * NS + NS], u[b % 2][:, k, a * P:a * P + P],
                                      part[:, k, 2 * P:2 * P + NS], start=(n == 0), stop=(n == 3 * CT - 1))
                            n += 1
                last.then_inc(s["f_cproj"], 1)

            def f_dtproj(b, i):
                pe.wait_ge(s["ld_dt"], 16)
                pe.wait_ge(s["f_dtin"], b + 1)
                take(f_ps, ("f_pos", 2 * b + i + 1))
                for j in range(2):
                    c = 2 * i + j
                    last = mm(pair(f_ps, j), w_dt[:, c * P:c * P + P], dt_in[:, :], start=True, stop=True)
                last.then_inc(s["f_dtproj"], 1)

            def spread_b(g):
                b, n = g // NP, g % NP
                pe.wait_ge(s["ld_bits"], 16)
                pe.wait_ge(s["f_bsplit"], b + 1)
                take(r_ps, ("b_copied", g + 1))
                for j in range(2):
                    last = mm(pair(r_ps, j), sel[:, 2 * n + j:2 * n + j + 1].to_broadcast([P, P]),
                              b_hi[b % 2][:, :], start=True, stop=True)
                last.then_inc(s["b_spread"], 1)

            def turn_h(k):
                g, n, a = k // 4, (k // 2) % 2, k % 2
                pe.wait_ge(s["scanned"], 4 * g + 4)
                take(h_t[k % 2], ("weighted", k + 1))
                for c in range(CT):
                    last = turn(h_t[k % 2][:, c * P:c * P + P],
                                h[:, (4 * g + c) % HRING, n, a * P:a * P + P], ident[:, :])
                last.then_inc(s["turned"], 1)

            def a_qk(b):
                pe.wait_ge(s["ld_att"], 16)
                take(r_ps, ("a_qk", 2 * b + 2))
                for i, w in enumerate((w_q, w_k)):
                    last = mm(pair(r_ps, i)[0:H, :], w[:, :], ctx_t[:, b, :], start=True, stop=True)
                last.then_inc(s["a_qkmm"], 1)

            def a_scores(b):
                pe.wait_ge(s["a_qk"], 2 * b + 2)
                take(r_ps, ("a_sc", b + 1))
                for a in range(TT):
                    last = mm(pair(r_ps, a), qk[:, 0, a * P:a * P + P], qk[:, 1, :], start=True, stop=True)
                last.then_inc(s["a_scmm"], 1)

            def o_turn(b, i):
                pe.wait_ge(s["weighted"], STEPS * (b + 1))
                take(r_ps, ("o_skip", 2 * b + i + 1))
                for j in range(2):
                    for a in range(TT):
                        c = 2 * i + j
                        last = turn(pair(r_ps, j)[:, a * P:a * P + P],
                                    acc[b % 2][:, a, c * P:c * P + P], ident[:, :])
                last.then_inc(s["o_turned"], 1)

            def o_proj(b, a):
                pe.wait_ge(s["o_gated"], 2 * b + 2)
                if a == 0:
                    pe.wait_ge(s["had_done"], 2)
                    take(r_ps, ("o_x1", b + 1))
                for c in range(CT):
                    last = mm(pair(r_ps, a), yd[:, c, a * P:a * P + P], w_oh[:, c, :],
                              start=(c == 0), stop=(c == CT - 1))
                last.then_inc(s["o_mm"], 1)

            def n_turn(b):
                pe.wait_ge(s["n_xf"], b + 1)
                take(r_ps, ("n_xft", b + 1))
                for k in range(DK):
                    for a in range(TT):
                        last = turn(pair(r_ps, k)[:, a * P:a * P + P], xf[:, a, k * P:k * P + P], ident[:, :])
                last.then_inc(s["n_turned"], 1)

            def g_logits(b):
                pe.wait_ge(s["ld_ffn"], 16)
                pe.wait_ge(s["n_xft"], b + 1)
                take(r_ps, ("g_lg", b + 1))
                for a in range(TT):
                    for k in range(DK):
                        last = mm(r_ps[:, a * E:a * E + E], xf_t[:, k, a * P:a * P + P], gate[:, k, :],
                                  start=(k == 0), stop=(k == DK - 1))
                last.then_inc(s["g_mm"], 1)

            def g_lora(b):
                take(r_ps, ("g_xa1", b + 1), ("g_xad", b + 1))
                for i, w in enumerate((la1, la3)):
                    for k in range(DK):
                        last = mm(pair(r_ps, i), w[:, k, :], xf_t[:, k, :], start=(k == 0), stop=(k == DK - 1))
                last.then_inc(s["g_xa"], 1)

            def g_turn_hot(b):
                pe.wait_ge(s["g_hot"], b + 1)
                take(f_ps, ("g_hcopy", b + 1))
                hb = f_ps[:, 0:256].bitcast(BF16).rearrange("p (s t) -> p s t", s=2)
                for i in range(2):
                    for a in range(TT):
                        last = turn(hb[:, i, a * P:a * P + P], hot[:, i, a, :], identb[:, :])
                last.then_inc(s["g_hturned"], 1)

            def g_turn_e(b):
                pe.wait_ge(s["g_exp"], b + 1)
                take(f_ps, ("g_ecopy", b + 1))
                for a in range(TT):
                    last = turn(pair(f_ps, 0)[:, a * P:a * P + P],
                                g_ex[:, a:a + 1].to_broadcast([P, P]), ident[:, :])
                last.then_inc(s["g_eturned"], 1)

            def ffn_base(b, f):
                pe.wait_ge(s["n_xft"], b + 1)
                bank, n = ffn_ps[f % 2], 2 * FT * b + 4 * (f // 2) + f % 2 + 1
                take(bank, ("h_copy", n), ("h_gate", n))
                for o, w in enumerate((w1, w3)):
                    for k in range(DK):
                        mm(pair(bank, o), w[:, k, f * P:f * P + P], xf_t[:, k, :],
                           start=(k == 0 and o == 0), stop=False, skip_group_check=True)

            def ffn_lora(b, j):
                f, i = ffn_half(j)
                bank, n = ffn_ps[f % 2], 2 * FT * b + j + 1
                if i == 0:
                    pe.wait_ge(s["g_xa1"], b + 1)
                else:
                    pe.wait_ge(s["g_xad"], b + 1)
                    take(bank, ("h_copy", n), ("h_gate", n))
                for o, lb in enumerate((lb1, lb3)):
                    last = mm(pair(bank, o), lb[:, f * P:f * P + P], (xad if i else xa1)[:, o, :],
                              start=False, stop=True, skip_group_check=True)
                last.then_inc(s["h_mm"], 1)

            def ffn_ranks(b, part):
                if part == 0:
                    take(ffn_ps[0], ("p_mask", b + 1))
                for f in range(2 * part, 2 * part + 2):
                    pe.wait_ge(s["h_act"], 2 * FT * b + 4 * (f // 2) + f % 2 + 3)
                    last = mm(ffn_ps[0][:, :], la2[:, f, :], aw[:, f, :, :], start=(f == 0), stop=(f == FT - 1))
                if part == FT // 2 - 1:
                    last.then_inc(s["p_mm"], 1)

            def ffn_down(b, part):
                a, half = part // 2, part % 2
                if part == 0:
                    take(ffn_ps[1], ("e_done", b + 1))
                pe.wait_ge(s["h_sum"], FT * b + 3 * half + 3)
                for f in range(3 * half, 3 * half + 3):
                    mm(pair(ffn_ps[1], a), aws[:, f, a * P:a * P + P], w2[:, f, :],
                       start=(part == 0 and f == 0), stop=False, skip_group_check=True)

            def ffn_down_lora(b):
                pe.wait_ge(s["p_sum"], b + 1)
                for a in range(TT):
                    last = mm(pair(ffn_ps[1], a), p_s[:, a * P:a * P + P], lb2[:, :],
                              start=False, stop=True, skip_group_check=True)
                last.then_inc(s["e_mm"], 1)

            def front(b, age):
                for i in due("pe.f_turn", age, b):
                    f_turn(b)
                for i in due("pe.f_proj_x", age, b):
                    f_proj_x(b, i)
                for i in due("pe.f_conv", age, b):
                    f_conv(b, i)
                for i in due("pe.f_proj_z", age, b):
                    f_proj_z(b, i)
                for i in due("pe.f_xproj", age, b):
                    f_xproj(b, i)
                for i in due("pe.f_cproj", age, b):
                    f_cproj(b)
                for i in due("pe.f_dtproj", age, b):
                    f_dtproj(b, i)

            def rest(b, age):
                for i in due("pe.a_qk", age, b):
                    a_qk(b)
                for i in due("pe.a_scores", age, b):
                    a_scores(b)
                for i in due("pe.o_turn", age, b):
                    o_turn(b, i)
                for i in due("pe.o_proj", age, b):
                    o_proj(b, i)
                for i in due("pe.n_turn", age, b):
                    n_turn(b)
                for i in due("pe.g_logits", age, b):
                    g_logits(b)
                for i in due("pe.g_lora", age, b):
                    g_lora(b)
                for i in due("pe.g_turn_hot", age, b):
                    g_turn_hot(b)
                for i in due("pe.g_turn_e", age, b):
                    g_turn_e(b)
                for f in due("pe.ffn_base", age, b):
                    ffn_base(b, f)
                for j in due("pe.ffn_lora", age, b):
                    ffn_lora(b, j)
                for i in due("pe.ffn_ranks", age, b):
                    ffn_ranks(b, i)
                for i in due("pe.ffn_down", age, b):
                    ffn_down(b, i)
                for i in due("pe.ffn_down_lora", age, b):
                    ffn_down_lora(b)

            for beat in range(FIRST, LAST):
                if (st := step(beat, TURN)) is not None:
                    turn_h(st)
                if (st := step(beat, SPREAD)) is not None and st % 4 == 0:
                    spread_b(st // 4)
                for b, age in rests(beat):
                    rest(b, age)
                for b, age in fronts(beat):
                    front(b, age)
                for _ in due("pe.hadamard_out", beat - FIRST):
                    hadamard_out()

        @block.scalar
        def _(act):
            go = nc.scalar.activation

            def split_wx():
                act.wait_ge(s["ld_x"], 16)
                go(w_x3[0][:, :, :], w_x[:, :, :], ACT.Copy).then_inc(s["wx_hi"], 1)
                act.wait_ge(s["wx_rest"], 1)
                go(w_x3[1][:, :, :], w_xr[:, :, :], ACT.Copy).then_inc(s["wx_mid"], 1)

            def hadamard_out():
                for i in range(2):
                    act.wait_ge(s["had_mm"], i + 1)
                    go(w_oh[:, 2 * i:2 * i + 2, :], pair(ffn_ps[i]), ACT.Copy,
                       scale=DI ** -0.5 * QS * 0.5).then_inc(s["had_done"], 1)

            def f_xn_copy(b):
                act.wait_ge(s["f_turned"], b + 1)
                go(xn_t[:, :, :], pair(f_ps), ACT.Copy).then_inc(s["f_xn_t"], 1)

            def f_xcopy(b, i):
                act.wait_ge(s["f_projx"], 2 * b + i + 1)
                if b:
                    act.wait_ge(s["f_dt"], 2 * b)
                act.wait_ge(s["pads_set"], 1)
                go(xq[:, 2 * i:2 * i + 2, :], pair(f_ps), ACT.Identity, bias=magic[:, 0:1],
                   scale=1.0 / QS).then_inc(s["f_xcopy"], 1)

            def f_q(b, i):
                act.wait_ge(s["f_clip"], 2 * b + i + 1)
                if b:
                    act.wait_ge(s["f_convmm"], 2 * b)
                go(q[:, 2 * i:2 * i + 2, TAPS - 1:TAPS - 1 + T], xq[:, 2 * i:2 * i + 2, :], ACT.Identity,
                   bias=magic[:, 1:2]).then_inc(s["f_quant"], 1)

            def f_ztanh(b, i):
                act.wait_ge(s["f_projz"], 2 * b + i + 1)
                act.wait_ge(s["f_silu"], 2 * b + 2)
                go(th[:, 2 * i:2 * i + 2, :], pair(r_ps), ACT.Tanh, scale=0.5).then_inc(s["f_ztanh"], 1)

            def f_tap(b, c):
                act.wait_ge(s["taps_set"], 1)
                act.wait_ge(s["f_quant"], 2 * b + c // 2 + 1)
                if b:
                    act.wait_ge(s["f_u"], 2 * b)
                go(v[:, c, :], q[:, c, TAPS - 1:TAPS - 1 + T], ACT.Identity, bias=conv_bs[:, c:c + 1],
                   scale=conv_ws[:, c, TAPS - 1:TAPS]).then_inc(s["f_tap"], 1)

            def f_vtanh(b, i):
                act.wait_ge(s["f_conv"], 2 * b + i + 1)
                if b:
                    act.wait_ge(s["f_z"], 2 * b)
                go(th[:, 2 * i:2 * i + 2, :], v[:, 2 * i:2 * i + 2, :], ACT.Tanh, scale=QS).then_inc(s["f_vtanh"], 1)

            def f_u(b, i):
                act.wait_ge(s["f_uclip"], 2 * b + i + 1)
                go(u[b % 2][:, 2 * i:2 * i + 2, :], v[:, 2 * i:2 * i + 2, :], ACT.Identity,
                   bias=magic[:, 1:2]).then_inc(s["f_u"], 1)

            def f_split(b):
                act.wait_ge(s["f_xproj"], 2 * b + 2)
                go(b_hi[b % 2][:, :], pair(f_ps, 1), ACT.Copy).then_inc(s["f_bhi"], 1)
                go(dt_in[:, :], pair(f_ps, 0), ACT.Copy, scale=QS).then_inc(s["f_dtin"], 1)

            def f_split2(b):
                act.wait_ge(s["f_brest"], b + 1)
                go(b_mid[64:96, :], b_rest[64:96, :], ACT.Copy)
                go(b_hi[b % 2][32:64, :], b_rest[32:64, :], ACT.Copy).then_inc(s["f_bmid"], 1)

            def f_ccopy(b):
                act.wait_ge(s["f_cproj"], b + 1)
                go(c_t[b % 2][:, :, :], f_ps[:, 0:TT * NS].rearrange("p (a n) -> p a n", a=TT),
                   ACT.Copy).then_inc(s["f_c"], 1)

            def f_abs(b, i):
                act.wait_ge(s["f_dtproj"], 2 * b + i + 1)
                act.wait_ge(s["f_z"], 2 * b + 2)
                for j in range(2):
                    c = 2 * i + j
                    last = go(dt_abs[:, c, :], pair(f_ps, j), ACT.Abs, bias=dt_bias[:, c:c + 1])
                last.then_inc(s["f_abs"], 1)
                for j in range(2):
                    c = 2 * i + j
                    last = go(dt_pos[:, c, :], pair(f_ps, j), ACT.Relu, bias=dt_bias[:, c:c + 1])
                last.then_inc(s["f_pos"], 1)

            def f_exp(b, i):
                act.wait_ge(s["f_abs"], 2 * b + i + 1)
                o = dt_abs[:, 2 * i:2 * i + 2, :]
                go(o, o, ACT.Exp, scale=-1.0).then_inc(s["f_exp"], 1)

            def f_softplus(b):
                act.wait_ge(s["f_exp"], 2 * b + 2)
                for i in range(2):
                    o = dt_abs[:, 2 * i:2 * i + 2, :]
                    go(o, o, ACT.Ln, bias=1.0).then_inc(s["f_ln"], 1)

            def copy_b(g):
                act.wait_ge(s["b_spread"], g + 1)
                if g >= BRING:
                    act.wait_ge(s["bu_ready"], 4 * (g - BRING + 1))
                go(b_rep[:, g % BRING, :, :], pair(r_ps), ACT.Copy).then_inc(s["b_copied"], 1)

            def decays(k):
                b, n, c = k // STEPS, (k // 4) % NP, k % 4
                act.wait_ge(s["f_dt"], 2 * b + c // 2 + 1)
                act.wait_ge(s["pads_set"], 1)
                if k >= 2:
                    act.wait_ge(s["scanned"], k - 1)
                for j in range(2):
                    last = go(pair(decay[k % 2], j)[:, 1:T], dt[b % 2][:, c, 1:T], ACT.Exp,
                              scale=a_log[:, c, 2 * n + j:2 * n + j + 1])
                last.then_inc(s["decay_ready"], 1)

            def a_qk(b):
                act.wait_ge(s["a_qkmm"], b + 1)
                for i in range(2):
                    go(qk[:, i, :], pair(r_ps, i)[0:H, :], ACT.Identity,
                       bias=b_qk[:, i:i + 1]).then_inc(s["a_qk"], 1)

            def a_scores(b):
                act.wait_ge(s["a_scmm"], b + 1)
                if b:
                    act.wait_ge(s["a_x2"], b)
                go(sc[:, :, :], pair(r_ps), ACT.Copy, scale=H ** -0.5).then_inc(s["a_sc"], 1)

            def a_probs(b):
                act.wait_ge(s["a_max"], b + 1)
                for a in range(TT):
                    last = go(sc[:, a, :], sc[:, a, :], ACT.Exp, bias=a_nm[:, a:a + 1],
                              accum_out=a_sum[:, a:a + 1])
                last.then_inc(s["a_exp"], 1)

            def n_copy(b):
                act.wait_ge(s["n_turned"], b + 1)
                go(xf_t[:, :, :], pair(r_ps), ACT.Copy).then_inc(s["n_xft"], 1)

            def g_exp(b):
                act.wait_ge(s["g_diff"], b + 1)
                go(g_ex[:, :], g_d[:, :], ACT.Exp).then_inc(s["g_exp"], 1)

            def g_hcopy(b):
                act.wait_ge(s["g_hturned"], b + 1)
                go(hot_t[:, :, :], f_ps[:, 0:256].bitcast(BF16).rearrange("p (s t) -> p s t", s=2),
                   ACT.Copy).then_inc(s["g_hcopy"], 1)

            def g_ecopy(b):
                act.wait_ge(s["g_eturned"], b + 1)
                go(e_rep[:, :], pair(f_ps, 0), ACT.Copy).then_inc(s["g_ecopy"], 1)

            def ffn_act(b, j):
                (f, _), n = ffn_half(j), 2 * FT * b
                bank = ffn_ps[f % 2]
                act.wait_ge(s["h_mm"], n + j + 1)
                if j == 0:
                    act.wait_ge(s["g_xad"], b + 1)
                    if b:
                        act.wait_ge(s["e_mm"], b)
                if n + j >= 2:
                    act.wait_ge(s["h_gate"], n + j - 1)
                go(ht[:, j % 2, :], pair(bank, 0), ACT.Tanh, scale=0.5).then_inc(s["h_tanh"], 1)
                if n + j >= 2:
                    act.wait_ge(s["h_act"], n + j - 1)
                go(h3[:, j % 2, :], pair(bank, 1), ACT.Copy).then_inc(s["h_copy"], 1)

            def front(b, age):
                for i in due("act.f_xn_copy", age, b):
                    f_xn_copy(b)
                for i in due("act.f_xcopy", age, b):
                    f_xcopy(b, i)
                for i in due("act.f_q", age, b):
                    f_q(b, i)
                for c in due("act.f_tap", age, b):
                    f_tap(b, c)
                for i in due("act.f_vtanh", age, b):
                    f_vtanh(b, i)
                for i in due("act.f_u", age, b):
                    f_u(b, i)
                for i in due("act.f_ztanh", age, b):
                    f_ztanh(b, i)
                for i in due("act.f_split", age, b):
                    f_split(b)
                for i in due("act.f_split2", age, b):
                    f_split2(b)
                for i in due("act.f_ccopy", age, b):
                    f_ccopy(b)
                for i in due("act.f_abs", age, b):
                    f_abs(b, i)
                for i in due("act.f_exp", age, b):
                    f_exp(b, i)
                for i in due("act.f_softplus", age, b):
                    f_softplus(b)

            def rest(b, age):
                for i in due("act.a_qk", age, b):
                    a_qk(b)
                for i in due("act.a_scores", age, b):
                    a_scores(b)
                for i in due("act.a_probs", age, b):
                    a_probs(b)
                for i in due("act.n_copy", age, b):
                    n_copy(b)
                for i in due("act.g_exp", age, b):
                    g_exp(b)
                for i in due("act.g_hcopy", age, b):
                    g_hcopy(b)
                for i in due("act.g_ecopy", age, b):
                    g_ecopy(b)
                for j in due("act.ffn_act", age, b):
                    ffn_act(b, j)

            for beat in range(FIRST, LAST):
                for _ in due("act.split_wx", beat - FIRST):
                    split_wx()
                if (st := step(beat, DECAY)) is not None:
                    decays(st)
                if (st := step(beat, COPY_B)) is not None and st % 4 == 0:
                    copy_b(st // 4)
                for b, age in rests(beat):
                    rest(b, age)
                for b, age in fronts(beat):
                    front(b, age)
                for _ in due("act.hadamard_out", beat - FIRST):
                    hadamard_out()

        @block.gpsimd
        def _(pool):
            tt, ts = nc.gpsimd.tensor_tensor, nc.gpsimd.tensor_scalar

            count = [0]

            def rstd(out, mv):
                count[0] += 1
                ts(out[:, :], mv[:, :, 1], EPS, None, ALU.add).then_inc(s["eps_added"], 1)
                pool.wait_ge(s["eps_added"], count[0])
                return tt(out[:, :], out[:, :], minus_half[:, :], ALU.pow)

            def hadamard4():
                pool.wait_ge(s["ld_out"], 16)
                tmp = yd
                tt(tmp[:, 0::2, :], w_out[:, 0::2, :], w_out[:, 1::2, :], ALU.add).then_inc(s["had_sum"], 1)
                tt(tmp[:, 1::2, :], w_out[:, 0::2, :], w_out[:, 1::2, :], ALU.subtract).then_inc(s["had_sum"], 1)
                pool.wait_ge(s["had_sum"], 2)
                tt(w_bf[:, 0:2, :], tmp[:, 0:2, :], tmp[:, 2:4, :], ALU.add).then_inc(s["had_sum"], 1)
                tt(w_bf[:, 2:4, :], tmp[:, 0:2, :], tmp[:, 2:4, :], ALU.subtract).then_inc(s["had_sum"], 1)

            def scan_input(k):
                b, g, c = k // STEPS, k // 4, k % 4
                pool.wait_ge(s["b_copied"], g + 1)
                pool.wait_ge(s["f_dtu"], 2 * b + c // 2 + 1)
                if k >= 3:
                    pool.wait_ge(s["scanned"], k - 2)
                tt(bu[:, k % 3, :, :], b_rep[:, g % BRING, :, :], dtu[b % 2][:, c:c + 1, :].to_broadcast([P, 2, T]),
                   ALU.mult).then_inc(s["bu_ready"], 1)

            def o_gate(b, i):
                pool.wait_ge(s["o_skip"], 2 * b + i + 1)
                tt(yd[:, 2 * i:2 * i + 2, :], yd[:, 2 * i:2 * i + 2, :], zs[b % 2][:, 2 * i:2 * i + 2, :],
                   ALU.mult).then_inc(s["o_gated"], 1)

            def ffn_pair(b, j):
                (f, i), n = ffn_half(j), 2 * FT * b
                pool.wait_ge(s["h_gate"], n + j + 1)
                pool.wait_ge(s["h_copy"], n + j + 1)
                if b:
                    pool.wait_ge(s["p_mm"], b)
                tt(aw[:, f, i, :], hg[:, j % 2, :], h3[:, j % 2, :], ALU.mult).then_inc(s["h_act"], 1)
                if i == 1:
                    pool.wait_ge(s["h_act"], n + j + 1)
                    pool.wait_ge(s["g_ecopy"], b + 1)
                    if b:
                        pool.wait_ge(s["e_mm"], b)
                    tt(aws[:, f, :], aw[:, f, 1, :], e_rep[:, :], ALU.mult).then_inc(s["h_scaled"], 1)
                    pool.wait_ge(s["h_scaled"], FT * b + f + 1)
                    tt(aws[:, f, :], aws[:, f, :], aw[:, f, 0, :], ALU.add).then_inc(s["h_sum"], 1)

            def hot_e(b):
                pool.wait_ge(s["g_xad"], b + 1)
                pool.wait_ge(s["g_ecopy"], b + 1)
                tt(hot_t[:, 1, :], hot_t[:, 1, :], e_rep[:, :], ALU.mult).then_inc(s["g_hot_e"], 1)

            def p_sum(b):
                pool.wait_ge(s["p_mask"], b + 1)
                tt(p_s, p_m[:, 0, :], p_m[:, 1, :], ALU.add).then_inc(s["p_sum"], 1)

            nc.gpsimd.memset(minus_half[:, :], -0.5).then_inc(s["half_set"], 1)
            pool.wait_ge(s["half_set"], 1)
            def rest(b, age):
                for i in due("pool.o_gate", age, b):
                    o_gate(b, i)
                for i in due("pool.a_rstd", age, b):
                    pool.wait_ge(s["a_var"], b + 1)
                    rstd(a_rs, a_mv).then_inc(s["a_rstd"], 1)
                for i in due("pool.n_rstd", age, b):
                    pool.wait_ge(s["n_var"], b + 1)
                    rstd(n_rs, n_mv).then_inc(s["n_rstd"], 1)
                for i in due("pool.hot_e", age, b):
                    hot_e(b)
                for j in due("pool.ffn_pair", age, b):
                    ffn_pair(b, j)
                for i in due("pool.p_sum", age, b):
                    p_sum(b)

            for beat in range(FIRST, LAST):
                if (st := step(beat, INPUT)) is not None:
                    scan_input(st)
                for b, age in rests(beat):
                    rest(b, age)
                for b, age in fronts(beat):
                    for i in due("pool.f_rstd", age, b):
                        pool.wait_ge(s["f_var"], b + 1)
                        rstd(f_rs, f_mv).then_inc(s["f_rstd"], 1)
                for _ in due("pool.hadamard4", beat - FIRST):
                    hadamard4()

        @block.vector
        def _(dve):
            ve = nc.vector
            tt, ts, stt = ve.tensor_tensor, ve.tensor_scalar, ve.scalar_tensor_tensor
            done = [0]

            def mark(ins):
                done[0] += 1
                ins.then_inc(s["dve_done"], 1)
                return done[0]

            def after(n):
                dve.wait_ge(s["dve_done"], n)

            def setup():
                ve.memset(magic[:, 0:1], MAGIC)
                ve.memset(magic[:, 1:2], -MAGIC)
                ve.memset(q[:, :, 0:TAPS - 1], 0.0)
                ve.memset(decay[0][:, :], 0.0)
                ve.memset(decay[1][:, :], 0.0).then_inc(s["pads_set"], 1)

            def setup_weights():
                dve.wait_ge(s["ld_small"], 16)
                ts(conv_ws[:, :, :], conv_w[:, :, :], 0.5, None, ALU.mult)
                ts(conv_bs[:, :], conv_b[:, :], 0.5 / QS, None, ALU.mult).then_inc(s["taps_set"], 1)

            def setup_conv():
                w, rest = conv_ws[:, :, 0:NT], conv_rest[:, :, :]
                dve.wait_ge(s["taps_set"], 1)
                dve.wait_ge(s["ld_bits"], 16)
                for i in range(3):
                    src = w if i == 0 else rest
                    after(mark(ve.tensor_copy(conv_part[:, :, i, :], src)))
                    if i < 2:
                        after(mark(tt(rest, src, conv_part[:, :, i, :], ALU.subtract)))
                for c in range(CT):
                    n = 3 * NT
                    tt(conv_d[:, c, :, :, :].rearrange("p i k m -> p (i k) m"),
                       conv_part[:, c, :, :].rearrange("p i (k o) -> p (i k) o", o=1).to_broadcast([P, n, P]),
                       identb.rearrange("p (o m) -> p o m", o=1).to_broadcast([P, n, P]),
                       ALU.mult).then_inc(s["conv_set"], 1)

            def setup_wx():
                dve.wait_ge(s["wx_hi"], 1)
                tt(w_xr[:, :, :], w_x[:, :, :], w_x3[0][:, :, :], ALU.subtract).then_inc(s["wx_rest"], 1)
                dve.wait_ge(s["wx_mid"], 1)
                dve.wait_ge(s["wx_rest"], 1)
                tt(w_x3[2][:, :, :], w_xr[:, :, :], w_x3[1][:, :, :], ALU.subtract).then_inc(s["wx_lo"], 1)

            def setup_masks():
                dve.wait_ge(s["ld_masks"], 16)
                for b in range(BATCH):
                    last = tt(masked[:, b, :, :], mask[:, :, :],
                              kmask[:, b:b + 1, :].to_broadcast([P, TT, T]), ALU.max)
                last.then_inc(s["masks_set"], 1)

            def norm_stats(src, st, mv, event):
                for a in range(TT):
                    last = ve.bn_stats(st[:, a, :], src[:, a, :])
                after(mark(last))
                for a in range(TT):
                    last = ve.bn_aggr(mv[:, a, :], st[:, a, :])
                last.then_inc(event, 1)

            def norm(dst, src, mv, rs):
                for a in range(TT):
                    last = ts(dst[:, a, :], src[:, a, :], mv[:, a, 0:1], rs[:, a:a + 1], ALU.subtract, ALU.mult)
                return last

            def f_stats(b):
                dve.wait_ge(s["ld_xt"], 16 * (b + 1))
                norm_stats(x_t, f_st, f_mv, s["f_var"])

            def f_norm(b):
                dve.wait_ge(s["f_rstd"], b + 1)
                norm(x_t, x_t, f_mv, f_rs).then_inc(s["f_xn"], 1)

            def f_clip(b, i):
                dve.wait_ge(s["f_xcopy"], 2 * b + i + 1)
                o = xq[:, 2 * i:2 * i + 2, :]
                ts(o, o, MAGIC + 127.0, MAGIC - 128.0, ALU.min, ALU.max).then_inc(s["f_clip"], 1)

            def f_gate(b, i):
                dve.wait_ge(s["f_ztanh"], 2 * b + i + 1)
                if b >= 2:
                    dve.wait_ge(s["o_gated"], 2 * (b - 1))
                stt(out=zs[b % 2][:, 2 * i:2 * i + 2, :], in0=th[:, 2 * i:2 * i + 2, :], scalar=1.0,
                    in1=pair(r_ps), op0=ALU.add, op1=ALU.mult).then_inc(s["f_z"], 1)

            def f_conv(b, i):
                dve.wait_ge(s["f_tap"], 4 * b + 2 * i + 2)
                dve.wait_ge(s["f_convmm"], 2 * b + i + 1)
                o = v[:, 2 * i:2 * i + 2, :]
                tt(o, pair(f_ps), o, ALU.add).then_inc(s["f_conv"], 1)

            def f_silu(b, i):
                dve.wait_ge(s["f_vtanh"], 2 * b + i + 1)
                o = v[:, 2 * i:2 * i + 2, :]
                stt(out=o, in0=th[:, 2 * i:2 * i + 2, :], scalar=1.0, in1=o, op0=ALU.add,
                    op1=ALU.mult).then_inc(s["f_silu"], 1)

            def f_uclip(b, i):
                dve.wait_ge(s["f_silu"], 2 * b + i + 1)
                o = v[:, 2 * i:2 * i + 2, :]
                ts(o, o, 127.0, MAGIC, ALU.min, ALU.add).then_inc(s["f_uclip"], 1)

            def f_split(b):
                dve.wait_ge(s["f_bhi"], b + 1)
                dve.wait_ge(s["f_dtin"], b + 1)
                tt(b_rest[:, :], pair(f_ps, 1), b_hi[b % 2][:, :], ALU.subtract).then_inc(s["f_brest"], 1)

            def f_split2(b):
                dve.wait_ge(s["f_bmid"], b + 1)
                tt(b_hi[b % 2][64:96, :], b_rest[64:96, :], b_mid[64:96, :], ALU.subtract).then_inc(s["f_bsplit"], 1)

            def f_dt(b, i):
                dve.wait_ge(s["f_ln"], 2 * b + i + 1)
                dve.wait_ge(s["f_pos"], 2 * b + i + 1)
                half = slice(2 * i, 2 * i + 2)
                tt(dt[b % 2][:, half, :], dt_pos[:, half, :], dt_abs[:, half, :], ALU.add).then_inc(s["f_dt"], 1)

            def f_dtu(b, i):
                dve.wait_ge(s["f_dt"], 2 * b + i + 1)
                dve.wait_ge(s["f_u"], 2 * b + i + 1)
                half = slice(2 * i, 2 * i + 2)
                stt(out=dtu[b % 2][:, half, :], in0=dt[b % 2][:, half, :], scalar=QS * QS,
                    in1=u[b % 2][:, half, :], op0=ALU.mult, op1=ALU.mult).then_inc(s["f_dtu"], 1)

            def scan(k):
                g, c = k // 4, k % 4
                dve.wait_ge(s["decay_ready"], k + 1)
                dve.wait_ge(s["bu_ready"], k + 1)
                if k >= HRING:
                    dve.wait_ge(s["turned"], 4 * ((k - HRING) // 4 + 1))
                ve.tensor_tensor_scan(h[:, k % HRING, :, :].rearrange("p n t -> p (n t)"), decay[k % 2][:, :],
                                      bu[:, k % 3, :, :].rearrange("p n t -> p (n t)"), 0.0,
                                      ALU.mult, ALU.add).then_inc(s["scanned"], 1)

            def weigh(k):
                b, n, a = k // STEPS, 2 * ((k // 4) % NP) + (k // 2) % 2, k % 2
                dst, src, c = acc[b % 2][:, a, :], h_t[k % 2][:, :], c_t[b % 2][:, a, n:n + 1]
                dve.wait_ge(s["turned"], k + 1)
                dve.wait_ge(s["f_c"], b + 1)
                if n == 0:
                    if b >= 2:
                        dve.wait_ge(s["o_turned"], 2 * (b - 1))
                    ts(dst, src, c, None, ALU.mult).then_inc(s["weighted"], 1)
                else:
                    dve.wait_ge(s["weighted"], k - 1)
                    stt(out=dst, in0=src, scalar=c, in1=dst, op0=ALU.mult, op1=ALU.add).then_inc(s["weighted"], 1)

            def o_skip(b, i):
                dve.wait_ge(s["o_turned"], 2 * b + i + 1)
                for j in range(2):
                    c = 2 * i + j
                    last = stt(out=yd[:, c, :], in0=u[b % 2][:, c, :], scalar=d_skip[:, c:c + 1],
                               in1=pair(r_ps, j), op0=ALU.mult, op1=ALU.add)
                last.then_inc(s["o_skip"], 1)

            def o_x1(b):
                dve.wait_ge(s["o_mm"], 2 * b + 2)
                dve.wait_ge(s["ld_res"], 16 * (b + 1))
                tt(x1[:, :, :], pair(r_ps), x_res[:, :, :], ALU.add).then_inc(s["o_x1"], 1)

            def a_stats(b):
                dve.wait_ge(s["o_x1"], b + 1)
                norm_stats(x1, a_st, a_mv, s["a_var"])

            def a_gate(b):
                dve.wait_ge(s["a_rstd"], b + 1)
                dve.wait_ge(s["a_sc"], b + 1)
                n = mark(norm(qc, x1, a_mv, a_rs))
                after(n)
                tt(sc[:, :, :], sc[:, :, :], qc[:, :, :], ALU.mult).then_inc(s["a_gated"], 1)

            def a_mask(b):
                dve.wait_ge(s["a_gated"], b + 1)
                dve.wait_ge(s["masks_set"], 1)
                after(mark(stt(out=sc[:, :, :], in0=masked[:, b, :, :], scalar=MASKED, in1=sc[:, :, :],
                               op0=ALU.mult, op1=ALU.add)))
                after(mark(ve.tensor_reduce(a_mx[:, :], sc[:, :, :], AX.X, ALU.max)))
                ts(a_nm[:, :], a_mx[:, :], -1.0, None, ALU.mult).then_inc(s["a_max"], 1)

            def a_x2(b):
                dve.wait_ge(s["a_exp"], b + 1)
                after(mark(ve.reciprocal(a_rec[:, :], a_sum[:, :])))
                if b >= 2:
                    dve.wait_ge(s["stored"], 16 * (b - 1))
                for a in range(TT):
                    last = stt(out=x2[b % 2][:, a, :], in0=sc[:, a, :], scalar=a_rec[:, a:a + 1], in1=x1[:, a, :],
                               op0=ALU.mult, op1=ALU.add)
                last.then_inc(s["a_x2"], 1)

            def n_stats(b):
                dve.wait_ge(s["a_x2"], b + 1)
                norm_stats(x2[b % 2], n_st, n_mv, s["n_var"])

            def n_norm(b):
                dve.wait_ge(s["n_rstd"], b + 1)
                norm(xf, x2[b % 2], n_mv, n_rs).then_inc(s["n_xf"], 1)

            def g_top(b):
                dve.wait_ge(s["g_mm"], b + 1)
                ve.tensor_copy(lg[:, :, :], r_ps[:, 0:TT * E].rearrange("p (a e) -> p a e", a=TT)).then_inc(
                    s["g_lg"], 1)
                dve.wait_ge(s["g_lg"], b + 1)
                for a in range(TT):
                    last = ve.max(out=top[:, a, :], in_=lg[:, a, :])
                after(mark(last))
                tt(g_d[:, :], top[:, :, 1], top[:, :, 0], ALU.subtract).then_inc(s["g_diff"], 1)

            def g_hot(b):
                for a in range(TT):
                    last = ve.max_index(out=topi[:, a, :], in_max=top[:, a, :], in_values=lg[:, a, :])
                after(mark(last))
                after(mark(ve.tensor_copy(topf[:, :, :], topi[:, :, :])))
                for i in range(2):
                    for a in range(TT):
                        last = ts(hot[:, i, a, :], rank_expert[:, :], topf[:, a, i:i + 1], None, ALU.is_equal)
                last.then_inc(s["g_hot"], 1)

            def g_weights(b):
                dve.wait_ge(s["g_exp"], b + 1)
                after(mark(ts(g_one[:, :], g_ex[:, :], 2.0, 2.0, ALU.mult, ALU.add)))
                after(mark(ve.reciprocal(g_w[:, b % 2, :], g_one[:, :])))

            def g_select(b):
                dve.wait_ge(s["g_hcopy"], b + 1)
                dve.wait_ge(s["g_xa"], b + 1)
                if b:
                    dve.wait_ge(s["p_sum"], b)
                n = mark(tt(hot_d, hot_t[:, 1, :], hot_t[:, 0, :], ALU.subtract))
                for o in range(2):
                    last = stt(out=xa1[:, o, :], in0=pair(r_ps, o), scalar=2.0, in1=hot_t[:, 0, :],
                               op0=ALU.mult, op1=ALU.mult)
                last.then_inc(s["g_xa1"], 1)
                after(n)
                for o in range(2):
                    last = stt(out=xad[:, o, :], in0=pair(r_ps, o), scalar=2.0, in1=hot_d,
                               op0=ALU.mult, op1=ALU.mult)
                last.then_inc(s["g_xad"], 1)

            def ffn_gate(b, j):
                (f, _), n = ffn_half(j), 2 * FT * b
                dve.wait_ge(s["h_tanh"], n + j + 1)
                dve.wait_ge(s["h_copy"], n + j + 1)
                if n + j >= 2:
                    dve.wait_ge(s["h_act"], n + j - 1)
                stt(out=hg[:, j % 2, :], in0=ht[:, j % 2, :], scalar=1.0, in1=pair(ffn_ps[f % 2], 0),
                    op0=ALU.add, op1=ALU.mult).then_inc(s["h_gate"], 1)

            def p_mask(b):
                dve.wait_ge(s["p_mm"], b + 1)
                dve.wait_ge(s["g_hot_e"], b + 1)
                stt(out=p_m[:, :, :], in0=pair(ffn_ps[0]), scalar=2.0, in1=hot_t[:, :, :], op0=ALU.mult,
                    op1=ALU.mult).then_inc(s["p_mask"], 1)

            def e_out(b):
                dve.wait_ge(s["e_mm"], b + 1)
                for a in range(TT):
                    o = x2[b % 2][:, a, :]
                    last = stt(out=o, in0=pair(ffn_ps[1], a), scalar=g_w[:, b % 2, a:a + 1], in1=o,
                               op0=ALU.mult, op1=ALU.add)
                last.then_inc(s["e_done"], 1)

            setup()

            def front(b, age):
                for i in due("dve.f_stats", age, b):
                    f_stats(b)
                for i in due("dve.f_norm", age, b):
                    f_norm(b)
                for i in due("dve.f_clip", age, b):
                    f_clip(b, i)
                for i in due("dve.f_conv", age, b):
                    f_conv(b, i)
                for i in due("dve.f_silu", age, b):
                    f_silu(b, i)
                for i in due("dve.f_uclip", age, b):
                    f_uclip(b, i)
                for i in due("dve.f_gate", age, b):
                    f_gate(b, i)
                for i in due("dve.f_split", age, b):
                    f_split(b)
                for i in due("dve.f_split2", age, b):
                    f_split2(b)
                for i in due("dve.f_dt", age, b):
                    f_dt(b, i)
                for i in due("dve.f_dtu", age, b):
                    f_dtu(b, i)

            def rest(b, age):
                for i in due("dve.o_skip", age, b):
                    o_skip(b, i)
                for i in due("dve.o_x1", age, b):
                    o_x1(b)
                for i in due("dve.a_stats", age, b):
                    a_stats(b)
                for i in due("dve.a_gate", age, b):
                    a_gate(b)
                for i in due("dve.a_mask", age, b):
                    a_mask(b)
                for i in due("dve.a_x2", age, b):
                    a_x2(b)
                for i in due("dve.n_stats", age, b):
                    n_stats(b)
                for i in due("dve.n_norm", age, b):
                    n_norm(b)
                for i in due("dve.g_top", age, b):
                    g_top(b)
                for i in due("dve.g_hot", age, b):
                    g_hot(b)
                for i in due("dve.g_weights", age, b):
                    g_weights(b)
                for i in due("dve.g_select", age, b):
                    g_select(b)
                for j in due("dve.ffn_gate", age, b):
                    ffn_gate(b, j)
                for i in due("dve.p_mask", age, b):
                    p_mask(b)
                for i in due("dve.e_out", age, b):
                    e_out(b)

            for beat in range(FIRST, LAST):
                if (st := step(beat, 0)) is not None:
                    scan(st)
                if (st := step(beat, WEIGH)) is not None:
                    weigh(st)
                for b, age in rests(beat):
                    rest(b, age)
                for b, age in fronts(beat):
                    front(b, age)
                for _ in due("dve.setup_weights", beat - FIRST):
                    setup_weights()
                for _ in due("dve.setup_conv", beat - FIRST):
                    setup_conv()
                for _ in due("dve.setup_wx", beat - FIRST):
                    setup_wx()
                for _ in due("dve.setup_masks", beat - FIRST):
                    setup_masks()


def kernel(**inputs):
    import numpy as np
    import ml_dtypes
    import concourse.bacc as bacc
    from concourse.bass_utils import run_bass_kernel_spmd

    a = {k: np.asarray(v) for k, v in inputs.items()}

    def rows(w):
        return w.reshape(-1, P, w.shape[-1]).transpose(1, 0, 2)

    def col(vec):
        return vec.reshape(-1, P).T

    def pad(w, axis):
        widths = [(0, 0)] * w.ndim
        widths[axis] = (0, FT * P - FF)
        return np.pad(w, widths)

    w_x = a["L0_attn_W_x"].T
    wide = np.zeros((DI, 2 * P + NS), w_x.dtype)
    wide[:, 0:P] = w_x[:, 0:P]
    for i in range(3):
        wide[:, P + 32 * i:P + 32 * i + NS] = w_x[:, P:P + NS]
    wide[:, 2 * P:] = w_x[:, P + NS:]

    ident = np.eye(P, dtype=np.float32)
    had = np.ones((1, 1), np.float32)
    while had.shape[0] < P:
        had = np.block([[had, had], [had, -had]])
    sel = np.zeros((P, NS), ml_dtypes.bfloat16)
    for n in range(NS):
        for i in range(3):
            sel[32 * i + n, n] = 1
    rank_expert = np.repeat(np.arange(E, dtype=np.float32), R)[None, :].repeat(P, 0)

    def packed(*parts):
        return np.concatenate([p.reshape(p.shape[0], -1) for p in parts], 1)

    arrays = {
        "x": a["x"],
        "small": packed(ident, a["L0_attn_conv_w"].reshape(CT, P, TAPS).transpose(1, 0, 2),
                        col(a["L0_attn_conv_b"]), col(a["L0_attn_dt_bias"]),
                        a["L0_attn_A"].reshape(CT, P, NS).transpose(1, 0, 2), col(a["L0_attn_D"])),
        "w_in": rows(a["L0_attn_W_in"].T),
        "w_x": rows(wide),
        "w_dt": a["L0_attn_W_dt"].T,
        "bits": packed(ident.astype(ml_dtypes.bfloat16), sel),
        "w_out": rows(a["L0_attn_W_out"].T),
        "had": had,
        "att": packed(a["ctx_512"].transpose(2, 0, 1), a["L0_xattn_Wq"].T, a["L0_xattn_Wk"].T,
                      np.stack([a["L0_xattn_bq"], a["L0_xattn_bk"]], 1)),
        "masks": np.concatenate([a["mask_SxS2_bk1"].reshape(TT, P, T).transpose(1, 0, 2),
                                 np.broadcast_to(a["mask_BxS2_bf0"][None], (P, BATCH, T))], 1),
        "ffn": packed(rows(a["L0_ffn_gate_w"].T), rows(a["L0_ffn_a1"].reshape(E * R, D).T),
                      rows(a["L0_ffn_a3"].reshape(E * R, D).T), rank_expert,
                      rows(pad(a["L0_ffn_w1"], 0).T), rows(pad(a["L0_ffn_w3"], 0).T),
                      pad(a["L0_ffn_b1"], 1).transpose(0, 2, 1).reshape(E * R, FT * P),
                      pad(a["L0_ffn_b3"], 1).transpose(0, 2, 1).reshape(E * R, FT * P),
                      rows(pad(a["L0_ffn_w2"], 1).T), rows(pad(a["L0_ffn_a2"], 2).reshape(E * R, FT * P).T),
                      a["L0_ffn_b2"].transpose(0, 2, 1).reshape(E * R, D)),
    }
    arrays = {f"in_{k}": np.ascontiguousarray(v) for k, v in arrays.items()}
    nc = bacc.Bacc("TRN2", target_bir_lowering=False, num_devices=1)
    t = {k[3:]: nc.dram_tensor(k, v.shape, mybir.dt.from_np(v.dtype), kind="ExternalInput").ap()
         for k, v in arrays.items()}
    t["out"] = nc.dram_tensor("out_0", (BATCH, T, D), F32, kind="ExternalOutput").ap()
    build(nc, t)
    r = run_bass_kernel_spmd(nc, [arrays], core_ids=[0])
    return r.results[0]["out_0"]
```
